# Optimizing a Trainium2 kernel written in Bass

```python
import numpy as np
import jax
import jax.numpy as jnp

def _softmax(x, axis=-1):
    return jax.nn.softmax(x, axis=axis)

def _gelu(x):
    return jax.nn.gelu(x, approximate=True)

def _silu(x):
    return jax.nn.silu(x)

def _sigmoid(x):
    return jax.nn.sigmoid(x)

def _layernorm(x, axis=-1, eps=1e-05):
    m = jnp.mean(x, axis=axis, keepdims=True)
    v = jnp.var(x, axis=axis, keepdims=True)
    return (x - m) / jnp.sqrt(v + eps)

def _scatter_add(tgt, idx, src, axis=0):
    return tgt.at[idx].add(src)

def _segment_sum(src, seg, n):
    return jax.ops.segment_sum(src, seg, n)
kernel_name = 'mk_seq_preln_d1_jaxref_r8_17adc1'

def setup_inputs(seed: int=0):
    np.random.seed(seed)
    _w = jnp.asarray

    def _L0_attn_setup():
        import jax, jax.numpy as jnp
        import numpy as np
        DIM = 128
        HEADS = 16
        HEAD_DIM = DIM // HEADS
        COLLAPSE_THRESHOLD = 0.27
        SHARPNESS = 15.0
        LN_EPS = 1e-05
        NORM_EPS = 1e-12

        def _layernorm(x, gamma, beta):
            mu = jnp.mean(x, axis=-1, keepdims=True)
            var = jnp.mean(jnp.square(x - mu), axis=-1, keepdims=True)
            return (x - mu) * jax.lax.rsqrt(var + LN_EPS) * gamma + beta

        def _l2_normalize(x):
            n = jnp.sqrt(jnp.sum(jnp.square(x), axis=-1, keepdims=True))
            return x / jnp.maximum(n, NORM_EPS)
        key = jax.random.key(seed)
        ks = jax.random.split(key, 9)
        B, T = (2, 256)
        s = 1.0 / np.sqrt(DIM)
        sh = 1.0 / np.sqrt(HEAD_DIM)
        return {'x': jax.random.normal(ks[0], (B, T, DIM), dtype=jnp.float32), 'w_q': jax.random.normal(ks[1], (DIM, DIM), dtype=jnp.float32) * s, 'w_k': jax.random.normal(ks[2], (DIM, DIM), dtype=jnp.float32) * s, 'w_v': jax.random.normal(ks[3], (DIM, DIM), dtype=jnp.float32) * s, 'g_q': jax.random.normal(ks[4], (HEAD_DIM,), dtype=jnp.float32) * sh, 'g_k': jax.random.normal(ks[5], (HEAD_DIM,), dtype=jnp.float32) * sh, 'w_o': jax.random.normal(ks[6], (DIM, DIM), dtype=jnp.float32) * s, 'b_o': jnp.zeros((DIM,), dtype=jnp.float32), 'gamma': jnp.ones((DIM,), dtype=jnp.float32), 'beta': jnp.zeros((DIM,), dtype=jnp.float32)}
    _L0_attn_in = _L0_attn_setup()

    def _L0_ffn_setup():
        import jax, jax.numpy as jnp
        import numpy as np
        B, S, D = (4, 256, 128)
        E, F = (8, 512)
        key = jax.random.key(seed)
        ks = jax.random.split(key, 5)
        x = jax.random.normal(ks[0], (B, S, D), dtype=jnp.float32)
        switch_w = jax.random.normal(ks[1], (D, E), dtype=jnp.float32) * D ** (-0.5)
        switch_b = jnp.zeros((E,), dtype=jnp.float32)
        w1 = jax.random.normal(ks[2], (E, D, F), dtype=jnp.float32) * D ** (-0.5)
        b1 = jnp.zeros((E, F), dtype=jnp.float32)
        w2 = jax.random.normal(ks[3], (E, F, D), dtype=jnp.float32) * F ** (-0.5)
        b2 = jnp.zeros((E, D), dtype=jnp.float32)
        return {'x': x, 'switch_w': switch_w, 'switch_b': switch_b, 'w1': w1, 'b1': b1, 'w2': w2, 'b2': b2}
    _L0_ffn_in = _L0_ffn_setup()
    _d = {'L0_attn_x': _L0_attn_in['x'], 'L0_attn_w_q': _L0_attn_in['w_q'], 'L0_attn_w_k': _L0_attn_in['w_k'], 'L0_attn_w_v': _L0_attn_in['w_v'], 'L0_attn_g_q': _L0_attn_in['g_q'], 'L0_attn_g_k': _L0_attn_in['g_k'], 'L0_attn_w_o': _L0_attn_in['w_o'], 'L0_attn_b_o': _L0_attn_in['b_o'], 'L0_attn_gamma': _L0_attn_in['gamma'], 'L0_attn_beta': _L0_attn_in['beta'], 'L0_ffn_switch_w': _L0_ffn_in['switch_w'], 'L0_ffn_switch_b': _L0_ffn_in['switch_b'], 'L0_ffn_w1': _L0_ffn_in['w1'], 'L0_ffn_b1': _L0_ffn_in['b1'], 'L0_ffn_w2': _L0_ffn_in['w2'], 'L0_ffn_b2': _L0_ffn_in['b2']}
    _x0 = _d['L0_attn_x']
    _d['L0_attn_x'] = jax.random.normal(jax.random.fold_in(jax.random.key(seed), 1), (2, 2048, 128), dtype=_x0.dtype)
    del _x0
    return _d

def reference(L0_attn_x, L0_attn_w_q, L0_attn_w_k, L0_attn_w_v, L0_attn_g_q, L0_attn_g_k, L0_attn_w_o, L0_attn_b_o, L0_attn_gamma, L0_attn_beta, L0_ffn_switch_w, L0_ffn_switch_b, L0_ffn_w1, L0_ffn_b1, L0_ffn_w2, L0_ffn_b2):

    def _L0_attn_ref(x, w_q, w_k, w_v, g_q, g_k, w_o, b_o, gamma, beta):
        import jax, jax.numpy as jnp
        import numpy as np
        DIM = 128
        HEADS = 16
        HEAD_DIM = DIM // HEADS
        COLLAPSE_THRESHOLD = 0.27
        SHARPNESS = 15.0
        LN_EPS = 1e-05
        NORM_EPS = 1e-12

        def _layernorm(x, gamma, beta):
            mu = jnp.mean(x, axis=-1, keepdims=True)
            var = jnp.mean(jnp.square(x - mu), axis=-1, keepdims=True)
            return (x - mu) * jax.lax.rsqrt(var + LN_EPS) * gamma + beta

        def _l2_normalize(x):
            n = jnp.sqrt(jnp.sum(jnp.square(x), axis=-1, keepdims=True))
            return x / jnp.maximum(n, NORM_EPS)
        B, T, D = x.shape
        x_norm = _layernorm(x, gamma, beta)
        q = (x_norm @ w_q).reshape(B, T, HEADS, HEAD_DIM).transpose(0, 2, 1, 3)
        k = (x_norm @ w_k).reshape(B, T, HEADS, HEAD_DIM).transpose(0, 2, 1, 3)
        v = (x @ w_v).reshape(B, T, HEADS, HEAD_DIM).transpose(0, 2, 1, 3)
        q = _l2_normalize(q)
        k = _l2_normalize(k)
        align = jnp.einsum('bhqd,bhkd->bhqk', q, k)
        resonance = 0.5 + 0.5 * jnp.tanh((align - COLLAPSE_THRESHOLD) * SHARPNESS)
        gate_q = 0.25 + 0.75 * jax.nn.sigmoid(jnp.einsum('bhtd,d->bht', q, g_q))
        gate_k = 0.25 + 0.75 * jax.nn.sigmoid(jnp.einsum('bhtd,d->bht', k, g_k))
        modulation = resonance * gate_q[..., :, None] * gate_k[..., None, :]
        fused = jnp.einsum('bhqk,bhkd->bhqd', modulation, v)
        fused = fused.transpose(0, 2, 1, 3).reshape(B, T, HEADS * HEAD_DIM)
        return fused @ w_o + b_o

    def _L0_ffn_ref(x, switch_w, switch_b, w1, b1, w2, b2):
        import jax, jax.numpy as jnp
        import numpy as np
        B, S, D = (4, 256, 128)
        E, F = (8, 512)
        b, s, d = x.shape
        t = x.reshape(-1, d)
        logits = t @ switch_w + switch_b
        route_prob = jax.nn.softmax(logits, axis=-1)
        route_prob_max = jnp.max(route_prob, axis=-1)
        routes = jnp.argmax(route_prob, axis=-1)
        out = jnp.zeros_like(t)
        n_experts = w1.shape[0]
        for e in range(n_experts):
            h = jax.nn.gelu(t @ w1[e] + b1[e])
            y = h @ w2[e] + b2[e]
            mask = (routes == e)[:, None]
            out = jnp.where(mask, y, out)
        out = out * route_prob_max[:, None]
        return out.reshape(b, s, d)
    x = L0_attn_x
    x = x + _L0_attn_ref(_layernorm(x, axis=-1), L0_attn_w_q, L0_attn_w_k, L0_attn_w_v, L0_attn_g_q, L0_attn_g_k, L0_attn_w_o, L0_attn_b_o, L0_attn_gamma, L0_attn_beta)
    x = x + _L0_ffn_ref(_layernorm(x, axis=-1), L0_ffn_switch_w, L0_ffn_switch_b, L0_ffn_w1, L0_ffn_b1, L0_ffn_w2, L0_ffn_b2)
    return x

_drawn_inputs = setup_inputs


def setup_inputs(seed=0):
    import zlib

    import numpy as np

    out = dict(_drawn_inputs(seed))
    spreads = {'L0_attn_b_o': (0.0, 0.8),
     'L0_attn_gamma': (1.0, 0.2),
     'L0_attn_beta': (0.0, 0.1),
     'L0_ffn_switch_b': (0.0, 0.8),
     'L0_ffn_b1': (0.0, 0.8),
     'L0_ffn_b2': (0.0, 2.0)}
    factors = {'L0_ffn_switch_w': 4.919, 'L0_ffn_w1': 5.164, 'L0_ffn_w2': 4.703}
    for name, (base, spread) in spreads.items():
        noise = np.random.default_rng([zlib.crc32(name.encode()), seed]).standard_normal(out[name].shape)
        drawn = base * np.exp(spread * noise) if base else spread * noise
        out[name] = jnp.asarray(drawn.astype(out[name].dtype))
    for name, factor in factors.items():
        out[name] = (out[name] * factor).astype(out[name].dtype)
    return out
```

```python
from contextlib import ExitStack

import concourse.bass as bass
from concourse import mybir

ALU = mybir.AluOpType
ACT = mybir.ActivationFunctionType
AX = mybir.AxisListType
F32 = mybir.dt.float32
F16 = mybir.dt.float16
I32 = mybir.dt.int32

P = 128
CH = 512
TPC = CH // P
HD = 8
HG = 4
QR = P // HG
SHARP = 30.0
THRESHOLD = 0.27
SPLIT = 4096.0
LN_EPS = 1e-5
NORM_EPS2 = 1e-24
GELU_CUBE = 0.044715
GELU_SCALE = 1.5957691216057308
RSQRT_SEED = 0x5F3759DF
UNIT = 3
RING = 4

J_X1T, J_XNT, J_QK0, J_QK1, J_V, J_GATE, J_Q0, J_Q1, J_K0, J_K1 = range(10)
PROLOGUE_JOBS = 10
J_WO, J_LNT, J_LOGITS, J_RANK = range(4)
POST_JOBS = 4
J_TT, J_UP, J_DOWN = range(3)
FFN_JOBS = 3


def unit_plan(tiles):
    plan = []
    for base in range(0, tiles, 32):
        plan += [(base + UNIT * i, UNIT) for i in range(10)] + [(base + 30, 2)]
    return plan


def build(nc, x, w_q, w_k, w_v, g_q, g_k, w_o, b_o, gamma, beta, switch_w, switch_b, w1, b1, w2, b2, out):
    B, T, D = x.shape
    H = D // HD
    G = H // HG
    E, _, F = w1.shape
    FC = F // P
    N = B * T
    NCH = N // CH
    QC = T // CH
    KB = T // P
    NT = N // P + E - 1
    NT += NT % 2
    CAP = N
    MC = CAP // P
    RW = 2 * D + 1
    SLOTS = E * CAP + NT * P
    TILES = G * KB * HG
    CONSTS = 19
    WEIGHT_LOADS = 10 + HG
    PROLOGUE_STEPS = 48
    POST_STEPS = 31
    FFN_STEPS = 4
    plan = unit_plan(TILES)
    U = len(plan)
    UG = U // G
    unit_of = {t: u for u, (t0, n) in enumerate(plan) for t in range(t0, t0 + n)}

    x_tok = x.rearrange("b t d -> (b t) d")
    out_tok = out.rearrange("b t d -> (b t) d")

    with ExitStack() as ctx:
        def sb(name, shape, dt=F32):
            return ctx.enter_context(nc.sbuf_tensor(name, shape, dt))

        def sem(name):
            return ctx.enter_context(nc.semaphore(name))

        q_dram = nc.dram_tensor("q_split", (NCH * G * P, CH), F16, kind="Internal").ap()
        gate_dram = nc.dram_tensor("q_gates", (NCH * H, CH), F32, kind="Internal").ap()
        rows_dram = nc.dram_tensor("token_rows", (N, RW), F32, kind="Internal").ap()
        slot_dram = nc.dram_tensor("slot_token", (SLOTS, 1), I32, kind="Internal").ap()

        psum = ctx.enter_context(nc.psum_tensor("psum", [P, 8, CH], F32))
        acc = psum[:, 6, :]
        misc = psum[:, 7, :]
        misc16 = misc.bitcast(F16)

        ident = sb("ident", [P, P])
        ident16 = sb("ident16", [P, P], F16)
        upper = sb("upper", [P, P])
        ones = sb("ones", [P, P])
        bias_t = sb("bias_t", [P, 1])
        zero16 = sb("zero16", [P, CH], F16)
        iota_e = sb("iota_e", [P, E])
        iota_m = sb("iota_m", [P, MC])
        iota_t = sb("iota_t", [P, NT])
        iota_p = sb("iota_p", [P, 1])
        no_token = sb("no_token", [P, NT], I32)
        tok_step = sb("tok_step", [P, TPC], I32)
        tok_i = sb("tok_i", [P, NCH * TPC], I32)
        gam = sb("gam", [P, 1])
        bet = sb("bet", [P, 1])
        bet_rep = sb("bet_rep", [P, P])
        wqk = sb("wqk", [P, 2, D])
        wqk_g = sb("wqk_g", [P, 2, D])
        wv = sb("wv", [P, D])
        wo = sb("wo", [P, G, D])
        g_heads = sb("g_heads", [P, 2, HD])
        bo = sb("bo", [P, D])
        sw = sb("sw", [P, E])
        swb = sb("swb", [P, E])
        qk_beta = sb("qk_beta", [P, 2, D])

        xres = sb("xres", [P, (NCH + 1) * TPC * D])
        kw = sb("kw", [P, NCH * G * CH], F16)
        vw = sb("vw", [P, NCH * TPC * D])

        st = sb("st", [P, TPC, 6])
        mv = sb("mv", [P, TPC, 2])
        var4 = sb("var4", [P, TPC])
        rs4 = sb("rs4", [P, TPC])
        nt_a = sb("nt_a", [P, 2 * TPC * H])
        nt_b = sb("nt_b", [P, 2 * TPC * H])
        x1 = sb("x1", [P, TPC, D])
        xn = sb("xn", [P, TPC, D])
        x1t = sb("x1t", [P, CH])
        xnt = sb("xnt", [P, CH])
        qk = sb("qk", [P, 2, TPC, D])
        qkn = sb("qkn", [P, 2, TPC, D])
        ss = sb("ss", [P, 2 * TPC * H])
        inv = sb("inv", [P, 2 * TPC * H])
        gsum = sb("gsum", [P, 2 * TPC * H])
        gates = sb("gates", [P, 2, TPC, H])
        qs = sb("qs", [P, TPC * H, 4, HD], F16)
        ks = sb("ks", [P, TPC * H, 4, HD], F16)
        qt = sb("qt", [P, G, CH], F16)
        gate_t = sb("gate_t", [H, CH])

        qm = sb("qm", [P, H, CH], F16)
        gt = sb("gt", [P, G, CH])
        ring = sb("ring", [P, RING, UNIT, CH])
        ft = sb("ft", [P, G, CH])

        rows = sb("rows", [P, TPC, RW])
        tt = sb("tt", [P, CH])
        lg = sb("lg", [P, TPC, E])
        lmax = sb("lmax", [P, TPC])
        sp_ = sb("sig_pos", [P, TPC, E])
        sn_ = sb("sig_neg", [P, TPC, E])
        ex = sb("ex", [P, TPC, E])
        emax = sb("emax", [P, TPC])
        esum = sb("esum", [P, TPC])
        cand = sb("cand", [P, TPC, E])
        route = sb("route", [P, TPC])
        onehot = sb("onehot", [P, TPC, E])
        rank = sb("rank", [P, 2, TPC, E])
        run = sb("run", [P, E])
        live = sb("live", [P, 1])
        slot_f = sb("slot_f", [P, TPC])
        slot_i = sb("slot_i", [P, TPC], I32)

        grid = sb("grid", [P, E, MC])
        tiles_e = sb("tiles_e", [P, E])
        cum_e = sb("cum_e", [P, E])
        started = sb("started", [P, NT, E])
        began = sb("began", [P, NT, E])
        tile_e = sb("tile_e", [P, NT])
        tile_s = sb("tile_s", [P, NT])
        sidx = sb("sidx", [P, NT], I32)
        eid = sb("eid", [P, NT], I32)

        sidx_now = sb("sidx_now", [P, 2], I32)
        ids = sb("ids", [P, 2], I32)
        fr = sb("fr", [P, 2, RW])
        fw1 = sb("fw1", [P, 2, F])
        fw2 = sb("fw2", [P, 2, FC, D])
        fb1 = sb("fb1", [P, 2, FC])
        fb2 = sb("fb2", [P, 2, D])
        ftt = sb("ftt", [P, P])
        fh = sb("fh", [P, FC, P])
        fu = sb("fu", [P, FC, P])
        fs = sb("fs", [P, FC, P])
        fg = sb("fg", [P, FC, P])
        fo = sb("fo", [P, 2, D])

        loaded_x = sem("loaded_x")
        loaded_w = sem("loaded_w")
        const_made = sem("const_made")
        bias_made = sem("bias_made")
        tok_copied = sem("tok_copied")
        wo_cleared = sem("wo_cleared")
        no_token_made = sem("no_token_made")
        pool_turns = sem("pool_turns")
        rows_free = sem("rows_free")
        slots_cleared = sem("slots_cleared")
        weights_made = sem("weights_made")
        misc_full = sem("misc_full")
        misc_free = sem("misc_free")
        vec = sem("vector_step")
        x1_ready = sem("x1_ready")
        xn_ready = sem("xn_ready")
        gsum_ready = sem("gsum_ready")
        gsig_ready = sem("gsig_ready")
        gates_ready = sem("gates_ready")
        qs_ready = sem("qs_ready")
        ks_ready = sem("ks_ready")
        q_stored = sem("q_stored")
        gate_stored = sem("gate_stored")
        q_loaded = [sem(f"q_loaded{g}") for g in range(G)]
        gt_loaded = [sem(f"gt_loaded{g}") for g in range(G)]
        qm_cleared = sem("qm_cleared")
        scores_ready = sem("scores_ready")
        sig_done = sem("sig_done")
        pv_done = sem("pv_done")
        acc_free = sem("acc_free")
        ft_ready = sem("ft_ready")
        t_ready = sem("t_ready")
        d_ready = sem("d_ready")
        esig_ready = sem("esig_ready")
        onehot_ready = sem("onehot_ready")
        row_ready = sem("row_ready")
        rows_stored = sem("rows_stored")
        slots_stored = sem("slots_stored")
        sched_ready = sem("sched_ready")
        sidx_copied = sem("sidx_copied")
        ids_loaded = [sem(f"ids_loaded{r}") for r in range(2)]
        rows_loaded = [sem(f"rows_loaded{r}") for r in range(2)]
        fw_loaded = [sem(f"fw_loaded{r}") for r in range(2)]
        gelu_ready = sem("gelu_ready")
        gelu_arg = sem("gelu_arg")
        gelu_sig = sem("gelu_sig")
        fo_ready = sem("fo_ready")
        out_stored = [sem(f"out_stored{r}") for r in range(2)]

        POST0 = PROLOGUE_JOBS * NCH
        FFN0 = POST0 + POST_JOBS * (NCH + 1)

        block = ctx.enter_context(nc.Block())

        @block.sync
        def _(sp):
            for c in range(NCH):
                src = x_tok[c * CH:(c + 1) * CH, :].rearrange("(t p) d -> p t d", p=P)
                dst = xres[:, (c + 1) * CH:(c + 2) * CH].rearrange("p (t d) -> p t d", t=TPC)
                sp.dma_start(dst, src).then_inc(loaded_x, 16)

            def store_chunk(c):
                sp.wait_ge(misc_free, c * PROLOGUE_JOBS + (J_GATE + 3))
                sp.dma_start(gate_dram[bass.ds(c * H, H), :], gate_t[:]).then_inc(gate_stored, 16)
                sp.wait_ge(misc_free, c * PROLOGUE_JOBS + (J_Q1 + 3))
                sp.dma_start(q_dram[bass.ds(c * (G * P), G * P), :].rearrange("(g p) n -> p g n", p=P),
                             qt[:]).then_inc(q_stored, 16)

            with sp.Fori(0, NCH) as c:
                store_chunk(c)

            def load_q(s, g):
                for j in range(HG):
                    sp.dma_start(qm[QR * j:QR * (j + 1), g * HG + j, :],
                                 q_dram[bass.ds(s * (G * P) + (g * P + QR * j), QR), :]).then_inc(q_loaded[g], 16)

            def load_gates(s, g):
                for j in range(HG):
                    sp.dma_start(gt[QR * j:QR * (j + 1), g, :],
                                 gate_dram[bass.ds(s * H + (g * HG + j), 1), :].to_broadcast([QR, CH])
                                 ).then_inc(gt_loaded[g], 16)

            sp.wait_ge(q_stored, 16 * (NCH + 1))
            sp.wait_ge(gate_stored, 16 * (NCH + 1))
            sp.wait_ge(qm_cleared, 1)
            for g in range(G):
                load_q(0, g)
                load_gates(0, g)
            with sp.Fori(1, NCH) as s:
                for g in range(G):
                    sp.wait_ge(scores_ready, s * U + (UG * (g + 1) - U))
                    load_q(s, g)
                    sp.wait_ge(acc_free, s * G + (g + 2 - G))
                    load_gates(s, g)
            sp.wait_ge(scores_ready, (NCH - 1) * U + UG)
            load_q(NCH - 1, 0)

            sp.wait_ge(sched_ready, 1)
            with sp.Fori(0, NT // 2) as pair:
                i = pair * 2
                for r in range(2):
                    sp.wait_ge(misc_free, i * FFN_JOBS + (FFN0 + FFN_JOBS * (r - 1) + 2))
                    e = sp.value_load(eid[0:1, bass.ds(i + r, 1)], min_val=0, max_val=E - 1)
                    w1_rows = w1.rearrange("e d f -> (e d) f")
                    w2_rows = w2.rearrange("e (p c) d -> (e p) c d", c=FC)
                    b1_rows = b1.rearrange("e (p c) -> (e p) c", c=FC)
                    sp.dma_start(fw1[:, r, :], w1_rows[bass.ds(e * P, P), :]).then_inc(fw_loaded[r], 16)
                    sp.dma_start(fw2[:, r, :, :], w2_rows[bass.ds(e * P, P), :, :]).then_inc(fw_loaded[r], 16)
                    sp.dma_start(fb1[:, r, :], b1_rows[bass.ds(e * P, P), :]).then_inc(fw_loaded[r], 16)
                    sp.dma_start(fb2[:, r, :], b2[bass.ds(e, 1), :].to_broadcast([P, D])).then_inc(fw_loaded[r], 16)

        @block.gpsimd
        def _(pool):
            made = [0]

            def make(ins):
                made[0] += 1
                ins.then_inc(const_made, 1)

            make(pool.memset(ident[:], 0.0))
            make(pool.memset(ident16[:], 0.0))
            make(pool.memset(upper[:], 0.0))
            pool.wait_ge(const_made, made[0])
            for m in (ident, ident16):
                make(pool.affine_select(out=m[:], in_=m[:], compare_op=ALU.not_equal, fill=1.0, base=0,
                                        pattern=[[-1, P]], channel_multiplier=1))
            make(pool.affine_select(out=upper[:], in_=upper[:], compare_op=ALU.is_ge, fill=1.0, base=0,
                                    pattern=[[-1, P]], channel_multiplier=1))
            make(pool.memset(ones[:], 1.0))
            make(pool.memset(zero16[:], 0.0))
            make(pool.iota(iota_e[:], pattern=[[1, E]], base=0, channel_multiplier=0,
                           allow_small_or_imprecise_dtypes=True))
            make(pool.iota(iota_m[:], pattern=[[P, MC]], base=0, channel_multiplier=0,
                           allow_small_or_imprecise_dtypes=True))
            make(pool.iota(iota_t[:], pattern=[[1, NT]], base=0, channel_multiplier=0,
                           allow_small_or_imprecise_dtypes=True))
            make(pool.iota(iota_p[:], pattern=[[0, 1]], base=0, channel_multiplier=1,
                           allow_small_or_imprecise_dtypes=True))
            make(pool.iota(tok_i[:], pattern=[[P, NCH * TPC]], base=0, channel_multiplier=1))
            make(pool.memset(xres[:, 0:CH], 0.0))
            make(pool.memset(ft[:], 0.0))
            make(pool.memset(run[:], 0.0))
            make(pool.memset(live[:], 0.0))
            make(pool.memset(fr[:], 0.0))
            make(pool.memset(rows[:], 0.0))
            assert made[0] == CONSTS
            pool.memset(qm[:], 0.0).then_inc(qm_cleared, 1)
            pool.memset(no_token[:], N).then_inc(no_token_made, 1)
            pool.wait_ge(no_token_made, 1)
            for i in range(0, SLOTS // P, NT):
                n = min(NT, SLOTS // P - i)
                pool.dma_start(slot_dram[i * P:(i + n) * P, :].rearrange("(p n) c -> p (n c)", p=P),
                               no_token[:, 0:n]).then_inc(slots_cleared, 16)
            pool.wait_ge(slots_cleared, 16 * len(range(0, SLOTS // P, NT)))

            def wait(sem_, value):
                pool.wait_ge(sem_, value)
                pool.sem_inc(pool_turns, 1)

            with pool.Fori(0, NCH) as c:
                wait(row_ready, c + 2)
                pool.tensor_copy(tok_step[:], tok_i[:, bass.ds(c * TPC, TPC)]).then_inc(tok_copied, 1)
                wait(tok_copied, c + 1)
                pool.dma_start(rows_dram[bass.ds(c * CH, CH), :].rearrange("(t p) w -> p t w", p=P),
                               rows[:]).then_inc(rows_stored, 16)
                for t in range(TPC):
                    pool.indirect_dma_start(slot_dram[:, :], bass.IndirectOffsetOnAxis(ap=slot_i[:, t:t + 1], axis=0),
                                            tok_step[:, t:t + 1], None).then_inc(slots_stored, 16)
                wait(rows_stored, c * 16 + 16)
                wait(slots_stored, c * (16 * TPC) + 16 * TPC)
                pool.sem_inc(rows_free, 1)

            pool.wait_ge(sched_ready, 1)
            with pool.Fori(0, NT // 2) as pair:
                i = pair * 2
                for r in range(2):
                    pool.tensor_copy(sidx_now[:, r:r + 1], sidx[:, bass.ds(i + r, 1)]).then_inc(sidx_copied, 1)
                    wait(sidx_copied, i + (r + 1))
                    pool.indirect_dma_start(ids[:, r:r + 1], None, slot_dram[:, :],
                                            bass.IndirectOffsetOnAxis(ap=sidx_now[:, r:r + 1], axis=0)
                                            ).then_inc(ids_loaded[r], 16)
                    wait(ids_loaded[r], i * 8 + 16)
                    pool.indirect_dma_start(fr[:, r, :], None, rows_dram[:, :],
                                            bass.IndirectOffsetOnAxis(ap=ids[:, r:r + 1], axis=0),
                                            bounds_check=N - 1, oob_is_err=False).then_inc(rows_loaded[r], 16)
                for r in range(2):
                    wait(fo_ready, i + (r + 1))
                    pool.indirect_dma_start(out_tok[:, :], bass.IndirectOffsetOnAxis(ap=ids[:, r:r + 1], axis=0),
                                            fo[:, r, :], None,
                                            bounds_check=N - 1, oob_is_err=False).then_inc(out_stored[r], 16)
                for r in range(2):
                    wait(out_stored[r], i * 8 + 16)

        @block.scalar
        def _(act):
            act.dma_start(gam[:], gamma.rearrange("(p a) -> p a", a=1)).then_inc(loaded_w, 16)
            act.dma_start(bet[:], beta.rearrange("(p a) -> p a", a=1)).then_inc(loaded_w, 16)
            act.dma_start(wqk[:, 0, :], w_q).then_inc(loaded_w, 16)
            act.dma_start(wqk[:, 1, :], w_k).then_inc(loaded_w, 16)
            act.dma_start(wv[:], w_v).then_inc(loaded_w, 16)
            act.dma_start(g_heads[:, 0, :], g_q.rearrange("(a d) -> a d", a=1).to_broadcast([P, HD])).then_inc(loaded_w, 16)
            act.dma_start(g_heads[:, 1, :], g_k.rearrange("(a d) -> a d", a=1).to_broadcast([P, HD])).then_inc(loaded_w, 16)
            act.dma_start(bo[:], b_o.rearrange("(a d) -> a d", a=1).to_broadcast([P, D])).then_inc(loaded_w, 16)
            act.dma_start(sw[:], switch_w).then_inc(loaded_w, 16)
            act.dma_start(swb[:], switch_b.rearrange("(a d) -> a d", a=1).to_broadcast([P, E])).then_inc(loaded_w, 16)
            act.wait_ge(wo_cleared, 1)
            wo_heads = w_o.rearrange("(g j d) n -> j d g n", j=HG, d=HD)
            for j in range(HG):
                act.dma_start(wo[QR * j:QR * j + HD, :, :], wo_heads[j]).then_inc(loaded_w, 16)

            with act.Fori(0, NCH) as c:
                act.wait_ge(gsum_ready, c + 1)
                act.activation(gsum[:], gsum[:], ACT.Sigmoid).then_inc(gsig_ready, 1)

            def units(s, lo, hi):
                for u in range(lo, hi):
                    t0, n = plan[u]
                    act.wait_ge(scores_ready, s * U + (u + 1))
                    last = plan[(u - RING) % U]
                    kb_last = (last[0] + last[1] - 1) // HG
                    act.wait_ge(pv_done, s * (G * KB) + (kb_last + 1 + (G * KB if u >= RING else 0)))
                    b0 = (u % 2) * UNIT
                    act.activation(ring[:, u % RING, 0:n, :], psum[:, b0:b0 + n, :], ACT.Sigmoid,
                                   scale=SHARP / SPLIT ** 2, bias=bias_t[:]).then_inc(sig_done, 1)

            act.wait_ge(bias_made, 1)
            with act.Fori(0, NCH) as s:
                units(s, 0, 22)
                act.wait_ge(d_ready, s + 1)
                act.activation(sp_[:], lg[:], ACT.Sigmoid)
                act.activation(sn_[:], lg[:], ACT.Sigmoid, scale=-1.0).then_inc(esig_ready, 1)
                units(s, 22, U)
            act.wait_ge(d_ready, NCH + 1)
            act.activation(sp_[:], lg[:], ACT.Sigmoid)
            act.activation(sn_[:], lg[:], ACT.Sigmoid, scale=-1.0).then_inc(esig_ready, 1)

            with act.Fori(0, NT) as i:
                act.wait_ge(gelu_arg, i + 1)
                act.activation(fs[:], fu[:], ACT.Sigmoid, scale=GELU_SCALE).then_inc(gelu_sig, 1)

        @block.vector
        def _(dve):
            steps = [0]

            def link(ins, base=0):
                steps[0] += 1
                ins.then_inc(vec, 1)
                dve.wait_ge(vec, base + steps[0])

            def rsqrt(y, a, t, u, base):
                link(dve.tensor_scalar(t.bitcast(I32), a.bitcast(I32), 1, None, ALU.logical_shift_right), base)
                link(dve.tensor_scalar(y.bitcast(I32), t.bitcast(I32), -1.0, float(RSQRT_SEED), ALU.mult, ALU.add), base)
                for _ in range(3):
                    link(dve.scalar_tensor_tensor(t, y, -0.5, y, ALU.mult, ALU.mult), base)
                    link(dve.tensor_tensor(u, t, a, ALU.mult), base)
                    link(dve.scalar_tensor_tensor(y, u, 1.5, y, ALU.add, ALU.mult), base)

            def layernorm(dst, src, base, done=None):
                for t in range(TPC):
                    last = dve.bn_stats(st[:, t, :], src[:, t, :])
                link(last, base)
                m_e, m_o, v_e, v_o = st[:, :, 1], st[:, :, 4], st[:, :, 2], st[:, :, 5]
                dve.tensor_tensor(mv[:, :, 0], m_e, m_o, ALU.add)
                dve.tensor_tensor(mv[:, :, 1], m_e, m_o, ALU.subtract)
                link(dve.tensor_tensor(var4[:], v_e, v_o, ALU.add), base)
                dve.tensor_scalar(mv[:, :, 0], mv[:, :, 0], 0.5, None, ALU.mult)
                dve.scalar_tensor_tensor(mv[:, :, 1], mv[:, :, 1], 0.25, mv[:, :, 1], ALU.mult, ALU.mult)
                link(dve.tensor_scalar(var4[:], var4[:], 1.0 / D, LN_EPS, ALU.mult, ALU.add), base)
                link(dve.tensor_tensor(var4[:], var4[:], mv[:, :, 1], ALU.add), base)
                rsqrt(rs4[:], var4[:], nt_a[:, 0:TPC], nt_b[:, 0:TPC], base)
                for t in range(TPC):
                    last = dve.tensor_scalar(dst[:, t, :], src[:, t, :], mv[:, t, 0:1], rs4[:, t:t + 1],
                                             ALU.subtract, ALU.mult)
                return last

            dve.sem_inc(misc_free, 1)
            dve.sem_inc(acc_free, 1)
            dve.sem_inc(pv_done, G * KB)
            dve.sem_inc(q_stored, 16)
            dve.sem_inc(gate_stored, 16)
            dve.sem_inc(rows_free, 2)
            dve.memset(wo[:], 0.0).then_inc(wo_cleared, 1)
            dve.memset(bias_t[:], -SHARP * THRESHOLD).then_inc(bias_made, 1)
            dve.wait_ge(loaded_w, 16 * WEIGHT_LOADS)
            dve.wait_ge(const_made, CONSTS)
            dve.tensor_scalar(bet_rep[:], ones[:], bet[:], None, ALU.mult)
            dve.tensor_scalar(wqk_g[:].rearrange("p a d -> p (a d)"), wqk[:].rearrange("p a d -> p (a d)"), gam[:],
                              None, ALU.mult).then_inc(weights_made, 1)
            dve.wait_ge(misc_full, 1)
            dve.tensor_copy(qk_beta[:].rearrange("p a d -> p (a d)"), misc[:, 0:2 * D]).then_inc(misc_free, 1)
            dve.wait_ge(misc_free, 2)
            dve.wait_ge(loaded_x, 16 * NCH)

            def prologue(c, base):
                job = lambda j: c * PROLOGUE_JOBS + (j + 2)
                n0 = steps[0]
                xc = xres[:, bass.ds(c * CH + CH, CH)].rearrange("p (t d) -> p t d", t=TPC)
                layernorm(x1, xc, base).then_inc(x1_ready, 1)
                dve.wait_ge(x1_ready, c + 1)
                layernorm(xn, x1, base).then_inc(xn_ready, 1)
                dve.wait_ge(misc_full, job(J_X1T))
                dve.tensor_copy(x1t[:], misc).then_inc(misc_free, 1)
                dve.wait_ge(misc_full, job(J_XNT))
                dve.tensor_copy(xnt[:], misc).then_inc(misc_free, 1)
                for half, j in ((0, J_QK0), (1, J_QK1)):
                    dve.wait_ge(misc_full, job(j))
                    dve.tensor_tensor(qk[:, :, 2 * half:2 * half + 2, :].rearrange("p a t d -> p t a d"),
                                      misc.rearrange("p (t a d) -> p t a d", t=2, a=2),
                                      qk_beta[:].unsqueeze(1).to_broadcast([P, 2, 2, D]),
                                      ALU.add).then_inc(misc_free, 1)
                dve.wait_ge(misc_free, job(J_QK1) + 1)
                qk_h = qk[:].rearrange("p a t (h d) -> p (a t h) d", d=HD)
                qkn_h = qkn[:].rearrange("p a t (h d) -> p (a t h) d", d=HD)
                NH = 2 * TPC * H
                link(dve.tensor_tensor(qkn_h, qk_h, qk_h, ALU.mult), base)
                link(dve.tensor_reduce(ss[:], qkn_h, AX.X, ALU.add), base)
                link(dve.tensor_scalar(ss[:], ss[:], NORM_EPS2, None, ALU.max), base)
                rsqrt(inv[:], ss[:], nt_a[:], nt_b[:], base)
                link(dve.tensor_tensor(qkn_h, qk_h, inv[:].unsqueeze(2).to_broadcast([P, NH, HD]), ALU.mult), base)
                for a in range(2):
                    last = dve.tensor_tensor(qk[:, a].rearrange("p t (h d) -> p (t h) d", d=HD),
                                             qkn[:, a].rearrange("p t (h d) -> p (t h) d", d=HD),
                                             g_heads[:, a, :].unsqueeze(1).to_broadcast([P, TPC * H, HD]), ALU.mult)
                link(last, base)
                dve.tensor_reduce(gsum[:], qk_h, AX.X, ALU.add).then_inc(gsum_ready, 1)
                q3 = qkn[:, 0].rearrange("p t (h d) -> p (t h) d", d=HD)
                k3 = qkn[:, 1].rearrange("p t (h d) -> p (t h) d", d=HD)
                for i in (0, 1):
                    dve.tensor_scalar(qs[:, :, i, :], q3, SPLIT, None, ALU.mult)
                for i in (0, 2):
                    last = dve.tensor_scalar(ks[:, :, i, :], k3, SPLIT, None, ALU.mult)
                link(last, base)
                dve.scalar_tensor_tensor(qs[:, :, 2, :], q3, SPLIT, qs[:, :, 0, :], ALU.mult, ALU.subtract)
                link(dve.scalar_tensor_tensor(ks[:, :, 1, :], k3, SPLIT, ks[:, :, 0, :], ALU.mult, ALU.subtract), base)
                dve.tensor_copy(qs[:, :, 3, :], qs[:, :, 2, :]).then_inc(qs_ready, 1)
                dve.tensor_copy(ks[:, :, 3, :], ks[:, :, 1, :]).then_inc(ks_ready, 1)
                dve.wait_ge(gsig_ready, c + 1)
                dve.tensor_scalar(gates[:].rearrange("p a t h -> p (a t h)"), gsum[:], 0.75, 0.25,
                                  ALU.mult, ALU.add).then_inc(gates_ready, 1)
                dve.wait_ge(gates_ready, c + 1)
                dve.wait_ge(misc_full, job(J_V))
                dve.tensor_tensor(vw[:, bass.ds(c * CH, CH)].rearrange("p (n d) -> p n d", d=HD),
                                  misc.rearrange("p (n d) -> p n d", d=HD),
                                  gates[:, 1].rearrange("p t h -> p (t h)").unsqueeze(2).to_broadcast([P, TPC * H, HD]),
                                  ALU.mult).then_inc(misc_free, 1)
                dve.wait_ge(misc_full, job(J_GATE))
                dve.wait_ge(gate_stored, c * 16 + 16)
                dve.tensor_copy(gate_t[:], misc[0:H, :]).then_inc(misc_free, 1)
                for half, j in ((0, J_Q0), (1, J_Q1)):
                    dve.wait_ge(misc_full, job(j))
                    if half == 0:
                        dve.wait_ge(q_stored, c * 16 + 16)
                    dve.tensor_copy(qt[:, :, 2 * P * half:2 * P * (half + 1)].rearrange("p g (t n) -> p t g n", t=2),
                                    misc16.rearrange("p (t g n) -> p t g n", t=2, g=G)).then_inc(misc_free, 1)
                kc = kw[:, bass.ds(c * (G * CH), G * CH)].rearrange("p (g n) -> p g n", g=G)
                for half, j in ((0, J_K0), (1, J_K1)):
                    dve.wait_ge(misc_full, job(j))
                    dve.tensor_copy(kc[:, :, 2 * P * half:2 * P * (half + 1)].rearrange("p g (t n) -> p t g n", t=2),
                                    misc16.rearrange("p (t g n) -> p t g n", t=2, g=G)).then_inc(misc_free, 1)
                return steps[0] - n0

            with dve.Fori(0, NCH) as c:
                n = prologue(c, c * PROLOGUE_STEPS)
                assert n == PROLOGUE_STEPS, n
            base0 = (NCH - 1) * PROLOGUE_STEPS

            def take_group(s, g):
                dve.wait_ge(gt_loaded[g], s * (16 * HG) + 16 * HG)
                dve.wait_ge(pv_done, s * (G * KB) + (G * KB + KB * (g + 1)))
                dve.tensor_tensor(ft[:, g, :], acc, gt[:, g, :], ALU.mult).then_inc(acc_free, 1)

            def post_parts(s, base):
                job = lambda j: s * POST_JOBS + (POST0 + j + 2)
                x2 = rows[:, :, D:2 * D]
                tn = rows[:, :, 0:D]
                xc = xres[:, bass.ds(s * CH, CH)].rearrange("p (t d) -> p t d", t=TPC)

                def residual():
                    dve.wait_ge(misc_full, job(J_WO))
                    dve.wait_ge(rows_free, s + 1)
                    dve.tensor_tensor(x2, misc.rearrange("p (t d) -> p t d", t=TPC),
                                      bo[:].unsqueeze(1).to_broadcast([P, TPC, D]), ALU.add).then_inc(misc_free, 1)
                    dve.wait_ge(misc_free, job(J_WO) + 1)
                    link(dve.tensor_tensor(x2, x2, xc, ALU.add), base)
                    layernorm(tn, x2, base).then_inc(t_ready, 1)

                def logits():
                    dve.wait_ge(misc_full, job(J_LNT))
                    dve.tensor_copy(tt[:], misc).then_inc(misc_free, 1)
                    dve.wait_ge(misc_full, job(J_LOGITS))
                    dve.tensor_tensor(lg[:], misc[:, 0:TPC * E].rearrange("p (t e) -> p t e", e=E),
                                      swb[:].unsqueeze(1).to_broadcast([P, TPC, E]), ALU.add).then_inc(misc_free, 1)
                    dve.wait_ge(misc_free, job(J_LOGITS) + 1)
                    link(dve.tensor_reduce(lmax[:], lg[:], AX.X, ALU.max), base)
                    dve.tensor_tensor(lg[:], lg[:], lmax[:].unsqueeze(2).to_broadcast([P, TPC, E]),
                                      ALU.subtract).then_inc(d_ready, 1)

                def routes():
                    dve.wait_ge(esig_ready, s + 1)
                    link(dve.reciprocal(sn_[:], sn_[:]), base)
                    link(dve.tensor_tensor(ex[:], sp_[:], sn_[:], ALU.mult), base)
                    dve.tensor_reduce(esum[:], ex[:], AX.X, ALU.add)
                    link(dve.tensor_reduce(emax[:], ex[:], AX.X, ALU.max), base)
                    dve.tensor_tensor(cand[:], ex[:], emax[:].unsqueeze(2).to_broadcast([P, TPC, E]), ALU.is_ge)
                    link(dve.reciprocal(esum[:], esum[:]), base)
                    dve.tensor_tensor(rows[:, :, 2 * D:RW], emax[:].unsqueeze(2), esum[:].unsqueeze(2), ALU.mult)
                    link(dve.scalar_tensor_tensor(cand[:], cand[:], -float(E),
                                                  iota_e[:].unsqueeze(1).to_broadcast([P, TPC, E]),
                                                  ALU.mult, ALU.add), base)
                    link(dve.tensor_reduce(route[:], cand[:], AX.X, ALU.min), base)
                    link(dve.tensor_scalar(route[:], route[:], float(E), None, ALU.add), base)
                    dve.tensor_tensor(onehot[:], iota_e[:].unsqueeze(1).to_broadcast([P, TPC, E]),
                                      route[:].unsqueeze(2).to_broadcast([P, TPC, E]),
                                      ALU.is_equal).then_inc(onehot_ready, 1)
                    dve.wait_ge(onehot_ready, s + 1)

                def ranks():
                    dve.wait_ge(misc_full, job(J_RANK))
                    dve.tensor_copy(rank[:].rearrange("p a t e -> p (a t e)"),
                                    misc[:, 0:2 * TPC * E]).then_inc(misc_free, 1)
                    dve.wait_ge(misc_free, job(J_RANK) + 1)
                    for t in range(TPC):
                        dve.tensor_tensor(rank[:, 0, t, :], rank[:, 0, t, :], run[:], ALU.add)
                        link(dve.tensor_tensor(run[:], run[:], rank[:, 1, t, :], ALU.add), base)
                    link(dve.tensor_tensor(rank[:, 0], rank[:, 0], onehot[:], ALU.mult), base)
                    link(dve.tensor_reduce(slot_f[:], rank[:, 0], AX.X, ALU.add), base)
                    dve.tensor_scalar(run[:], run[:], live[:], None, ALU.mult)
                    link(dve.scalar_tensor_tensor(slot_f[:], route[:], float(CAP), slot_f[:], ALU.mult, ALU.add), base)
                    dve.memset(live[:], 1.0)
                    dve.tensor_copy(slot_i[:], slot_f[:]).then_inc(row_ready, 1)
                    dve.wait_ge(row_ready, s + 1)

                return residual, logits, routes, ranks

            with dve.Fori(0, NCH) as s:
                n0 = steps[0]
                base = s * POST_STEPS + base0
                residual, logits, routes, ranks = post_parts(s, base)
                residual()
                logits()
                routes()
                take_group(s, 0)
                ranks()
                take_group(s, 1)
                take_group(s, 2)
                take_group(s, 3)
                assert steps[0] - n0 == POST_STEPS, steps[0] - n0
            base0 += (NCH - 1) * POST_STEPS
            for part in post_parts(NCH, base0):
                part()

            b3 = lambda ap, shape, at: ap.unsqueeze(at).to_broadcast(shape)
            link(dve.tensor_tensor(grid[:], b3(run[:], [P, E, MC], 2), b3(iota_m[:], [P, E, MC], 1), ALU.is_gt), base0)
            link(dve.tensor_reduce(tiles_e[:], grid[:], AX.X, ALU.add), base0)
            link(dve.tensor_copy(cum_e[:], tiles_e[:]), base0)
            for e in range(1, E):
                link(dve.tensor_tensor(cum_e[:, e:e + 1], cum_e[:, e - 1:e], tiles_e[:, e:e + 1], ALU.add), base0)
            link(dve.tensor_tensor(started[:], b3(cum_e[:], [P, NT, E], 1), b3(iota_t[:], [P, NT, E], 2), ALU.is_le), base0)
            dve.tensor_reduce(tile_e[:], started[:], AX.X, ALU.add)
            link(dve.tensor_tensor(began[:], started[:], b3(tiles_e[:], [P, NT, E], 1), ALU.mult), base0)
            link(dve.tensor_reduce(tile_s[:], began[:], AX.X, ALU.add), base0)
            link(dve.tensor_tensor(tile_s[:], iota_t[:], tile_s[:], ALU.subtract), base0)
            link(dve.tensor_scalar(tile_s[:], tile_s[:], float(P), iota_p[:], ALU.mult, ALU.add), base0)
            link(dve.scalar_tensor_tensor(tile_s[:], tile_e[:], float(CAP), tile_s[:], ALU.mult, ALU.add), base0)
            dve.tensor_copy(sidx[:], tile_s[:])
            dve.tensor_scalar(eid[:], tile_e[:], float(E - 1), None, ALU.min).then_inc(sched_ready, 1)

            with dve.Fori(0, NT // 2) as pair:
                i = pair * 2
                n0 = steps[0]
                for r in range(2):
                    base = i * (FFN_STEPS // 2) + base0
                    job = lambda j: i * FFN_JOBS + (FFN0 + r * FFN_JOBS + j + 2)
                    dve.wait_ge(misc_full, job(J_TT))
                    dve.tensor_copy(ftt[:], misc[:, 0:P]).then_inc(misc_free, 1)
                    dve.wait_ge(misc_full, job(J_UP))
                    dve.wait_ge(fw_loaded[r], i * 32 + 64)
                    dve.tensor_tensor(fh[:], misc.rearrange("p (c n) -> p c n", c=FC),
                                      fb1[:, r, :].unsqueeze(2).to_broadcast([P, FC, P]), ALU.add).then_inc(misc_free, 1)
                    dve.wait_ge(misc_free, job(J_UP) + 1)
                    link(dve.tensor_tensor(fu[:], fh[:], fh[:], ALU.mult), base)
                    link(dve.tensor_scalar(fu[:], fu[:], GELU_CUBE, 1.0, ALU.mult, ALU.add), base)
                    dve.tensor_tensor(fu[:], fu[:], fh[:], ALU.mult).then_inc(gelu_arg, 1)
                    dve.wait_ge(gelu_sig, i + (r + 1))
                    dve.tensor_tensor(fg[:], fs[:], fh[:], ALU.mult).then_inc(gelu_ready, 1)
                    dve.wait_ge(misc_full, job(J_DOWN))
                    dve.wait_ge(rows_loaded[r], i * 8 + 16)
                    dve.tensor_tensor(fo[:, r, :], misc[:, 0:D], fb2[:, r, :], ALU.add).then_inc(misc_free, 1)
                    dve.wait_ge(misc_free, job(J_DOWN) + 1)
                    dve.scalar_tensor_tensor(fo[:, r, :], fo[:, r, :], fr[:, r, 2 * D:RW], fr[:, r, D:2 * D],
                                             ALU.mult, ALU.add).then_inc(fo_ready, 1)
                assert steps[0] - n0 == FFN_STEPS, steps[0] - n0

        @block.tensor
        def _(pe):
            pe.wait_ge(const_made, CONSTS)
            pe.matmul(acc, zero16[:, 0:P], zero16[:], start=True, stop=True)
            pe.wait_ge(weights_made, 1)
            pe.wait_ge(misc_free, 1)
            pe.matmul(misc[:, 0:2 * D], bet_rep[:], wqk[:].rearrange("p a d -> p (a d)"),
                      start=True, stop=True).then_inc(misc_full, 1)

            def prologue(c):
                def free(j):
                    pe.wait_ge(misc_free, c * PROLOGUE_JOBS + (j + 2))

                pe.wait_ge(x1_ready, c + 1)
                free(J_X1T)
                for t in range(TPC):
                    last = pe.transpose(misc[:, t * P:(t + 1) * P], x1[:, t, :], ident[:])
                last.then_inc(misc_full, 1)
                pe.wait_ge(xn_ready, c + 1)
                free(J_XNT)
                for t in range(TPC):
                    last = pe.transpose(misc[:, t * P:(t + 1) * P], xn[:, t, :], ident[:])
                last.then_inc(misc_full, 1)
                for half, j in ((0, J_QK0), (1, J_QK1)):
                    free(j)
                    for t in range(2):
                        tile = 2 * half + t
                        last = pe.matmul(misc[:, t * 2 * D:(t + 1) * 2 * D], xnt[:, tile * P:(tile + 1) * P],
                                         wqk_g[:].rearrange("p a d -> p (a d)"), start=True, stop=True)
                    last.then_inc(misc_full, 1)
                free(J_V)
                for t in range(TPC):
                    last = pe.matmul(misc[:, t * D:(t + 1) * D], x1t[:, t * P:(t + 1) * P], wv[:],
                                     start=True, stop=True)
                last.then_inc(misc_full, 1)
                pe.wait_ge(gates_ready, c + 1)
                free(J_GATE)
                for t in range(TPC):
                    last = pe.transpose(misc[0:H, t * P:(t + 1) * P], gates[:, 0, t, :], ident[:])
                last.then_inc(misc_full, 1)
                for src, made, jobs in ((qs, qs_ready, (J_Q0, J_Q1)), (ks, ks_ready, (J_K0, J_K1))):
                    pe.wait_ge(made, c + 1)
                    for half, j in enumerate(jobs):
                        free(j)
                        for t in range(2):
                            for g in range(G):
                                r0 = (2 * half + t) * H + g * HG
                                at = (t * G + g) * P
                                last = pe.transpose(misc16[:, at:at + P],
                                                    src[:, r0:r0 + HG, :, :].rearrange("p h c d -> p (h c d)"),
                                                    ident16[:])
                        last.then_inc(misc_full, 1)

            with pe.Fori(0, NCH) as c:
                prologue(c)
            pe.wait_ge(misc_free, NCH * PROLOGUE_JOBS + 2)

            def scores(b, s, u):
                over, v = divmod(u, U)
                t0, n = plan[v]
                if s is not None:
                    pe.wait_ge(sig_done, s * U + (u - 1))
                for i in range(n):
                    g, kb, j = (t0 + i) // (KB * HG), (t0 + i) // HG % KB, (t0 + i) % HG
                    if (t0 + i) % (KB * HG) == 0:
                        first = 16 * HG * (1 + over)
                        pe.wait_ge(q_loaded[g], first if s is None else s * (16 * HG) + first)
                    at = ((b * QC + kb // TPC) * G + g) * CH + kb % TPC * P
                    keys = kw[:, at:at + P]
                    if over and b + 1 < B:
                        keys = kw[:, bass.ds((s + 1) // QC * (QC * G * CH) + at, P)]
                    last = pe.matmul(psum[:, (u % 2) * UNIT + i, :], keys, qm[:, g * HG + j, :],
                                     start=True, stop=True)
                last.then_inc(scores_ready, 1)

            def values(b, s, g, kb):
                pe.wait_ge(sig_done, s * U + (unit_of[(g * KB + kb) * HG + HG - 1] + 1))
                if kb == 0:
                    pe.wait_ge(acc_free, s * G + (g + 1))
                for j in range(HG):
                    tile = (g * KB + kb) * HG + j
                    u = unit_of[tile]
                    at = (b * KB + kb) * D + (g * HG + j) * HD
                    last = pe.matmul(acc[QR * j:QR * j + HD, :], vw[:, at:at + HD],
                                     ring[:, u % RING, tile - plan[u][0], :],
                                     start=(kb == 0), stop=(kb == KB - 1), tile_position=(0, QR * j))
                last.then_inc(pv_done, 1)

            def post_jobs(s):
                def free(j):
                    pe.wait_ge(misc_free, s * POST_JOBS + (POST0 + j + 2))

                def project():
                    free(J_WO)
                    for t in range(TPC):
                        for g in range(G):
                            last = pe.matmul(misc[:, t * D:(t + 1) * D], ft[:, g, t * P:(t + 1) * P], wo[:, g, :],
                                             start=(g == 0), stop=(g == G - 1))
                    last.then_inc(misc_full, 1)

                def turn():
                    pe.wait_ge(t_ready, s + 1)
                    free(J_LNT)
                    for t in range(TPC):
                        last = pe.transpose(misc[:, t * P:(t + 1) * P], rows[:, t, 0:D], ident[:])
                    last.then_inc(misc_full, 1)

                def route():
                    free(J_LOGITS)
                    for t in range(TPC):
                        last = pe.matmul(misc[:, t * E:(t + 1) * E], tt[:, t * P:(t + 1) * P], sw[:],
                                         start=True, stop=True)
                    last.then_inc(misc_full, 1)

                def count():
                    pe.wait_ge(onehot_ready, s + 1)
                    free(J_RANK)
                    oh = onehot[:].rearrange("p t e -> p (t e)")
                    pe.matmul(misc[:, 0:TPC * E], upper[:], oh, start=True, stop=True)
                    pe.matmul(misc[:, TPC * E:2 * TPC * E], ones[:], oh, start=True, stop=True).then_inc(misc_full, 1)

                return project, turn, route, count

            scores(0, None, 0)
            scores(0, None, 1)
            for b in range(B):
                with pe.Fori(b * QC, (b + 1) * QC) as s:
                    project, turn, route, count = post_jobs(s)
                    for u in range(U):
                        scores(b, s, u + 2)
                        for q in range(G * KB):
                            if unit_of[q * HG + HG - 1] == u:
                                values(b, s, q // KB, q % KB)
                        if u == 4:
                            project()
                        if u == 12:
                            turn()
                        if u == 16:
                            route()
                        if u == 30:
                            count()
            pe.wait_ge(acc_free, NCH * G + 1)
            for part in post_jobs(NCH):
                part()

            with pe.Fori(0, NT // 2) as pair:
                i = pair * 2
                for r in range(2):
                    free = lambda j: pe.wait_ge(misc_free, i * FFN_JOBS + (FFN0 + r * FFN_JOBS + j + 2))
                    pe.wait_ge(rows_loaded[r], i * 8 + 16)
                    free(J_TT)
                    pe.transpose(misc[:, 0:P], fr[:, r, 0:D], ident[:]).then_inc(misc_full, 1)
                    pe.wait_ge(fw_loaded[r], i * 32 + 64)
                    free(J_UP)
                    for f in range(FC):
                        last = pe.matmul(misc[:, f * P:(f + 1) * P], fw1[:, r, f:F:FC], ftt[:], start=True, stop=True)
                    last.then_inc(misc_full, 1)
                    pe.wait_ge(gelu_ready, i + (r + 1))
                    free(J_DOWN)
                    for f in range(FC):
                        last = pe.matmul(misc[:, 0:D], fg[:, f, :], fw2[:, r, f, :], start=(f == 0), stop=(f == FC - 1))
                    last.then_inc(misc_full, 1)


_INS = ['L0_attn_x', 'L0_attn_w_q', 'L0_attn_w_k', 'L0_attn_w_v', 'L0_attn_g_q', 'L0_attn_g_k', 'L0_attn_w_o',
        'L0_attn_b_o', 'L0_attn_gamma', 'L0_attn_beta', 'L0_ffn_switch_w', 'L0_ffn_switch_b', 'L0_ffn_w1',
        'L0_ffn_b1', 'L0_ffn_w2', 'L0_ffn_b2']


def kernel(**inputs):
    import numpy as _np
    import concourse.bacc as _bacc
    from concourse import mybir as _mybir
    from concourse.bass_utils import run_bass_kernel_spmd as _run

    nc = _bacc.Bacc("TRN2", target_bir_lowering=False, num_devices=1)
    arrays, args = {}, []
    for name in _INS:
        a = _np.ascontiguousarray(inputs[name])
        arrays[f"in_{name}_dram"] = a
        args.append(nc.dram_tensor(f"in_{name}_dram", a.shape, _mybir.dt.from_np(a.dtype), kind="ExternalInput").ap())
    shape = arrays["in_L0_attn_x_dram"].shape
    out = nc.dram_tensor("out_0_dram", shape, _mybir.dt.float32, kind="ExternalOutput").ap()
    build(nc, *args, out)
    r = _run(nc, [arrays], core_ids=[0])
    return r.results[0]["out_0_dram"]
```

```python
from contextlib import ExitStack

import concourse.bass as bass
from concourse import mybir

ALU = mybir.AluOpType
ACT = mybir.ActivationFunctionType
AX = mybir.AxisListType
F32 = mybir.dt.float32
F16 = mybir.dt.float16
I32 = mybir.dt.int32

P = 128
CH = 512
TPC = CH // P
HD = 8
HG = 4
QR = P // HG
SHARP = 30.0
THRESHOLD = 0.27
SPLIT = 4096.0
LN_EPS = 1e-5
NORM_EPS2 = 1e-24
GELU_CUBE = 0.044715
GELU_SCALE = 1.5957691216057308
RSQRT_SEED = 0x5F3759DF
UNIT = 2
BANKS = 3
RING = 16

J_X1T, J_XNT, J_QK0, J_QK1, J_V, J_GATE, J_Q0, J_Q1, J_K0, J_K1 = range(10)
PROLOGUE_JOBS = 10
J_WO, J_LNT, J_LOGITS, J_RANK = range(4)
POST_JOBS = 4

POST_AT = (5, 15, 17, 38)
PROLOGUE_AT = (50, 58, 59, 60, 61, 80, 81, 82, 83, 84)
ROUTES_AT = 23
GATES_AT = 75
AHEAD = 3
ROWS_BUFS = 4
IDS_BUFS = 8


def unit_plan(tiles):
    plan = [(t, UNIT) for t in range(0, tiles, UNIT)]
    while len(plan) % BANKS:
        at = max(i for i, (_, n) in enumerate(plan) if n == UNIT)
        t = plan[at][0]
        plan[at:at + 1] = [(t, 1), (t + 1, 1)]
    return plan


def build(nc, x, w_q, w_k, w_v, g_q, g_k, w_o, b_o, gamma, beta, switch_w, switch_b, w1, b1, w2, b2, out):
    B, T, D = x.shape
    H = D // HD
    G = H // HG
    E, _, F = w1.shape
    FC = F // P
    N = B * T
    NCH = N // CH
    QC = T // CH
    KB = T // P
    NT = -(-(N // P + E - 1) // IDS_BUFS) * IDS_BUFS
    NS = NT + AHEAD
    CAP = N
    MC = CAP // P
    RW = 2 * D + 1
    EW = FC * D + FC + D
    SLOTS = E * CAP + NS * P
    TILES = G * KB * HG
    CONSTS = 18
    WEIGHT_LOADS = 10 + HG
    PROLOGUE_STEPS = 48
    POST_STEPS = 31
    LOOP_STEPS = (POST_STEPS + PROLOGUE_STEPS, POST_STEPS)
    LOOP_JOBS = (POST_JOBS + PROLOGUE_JOBS, POST_JOBS)
    plan = unit_plan(TILES)
    U = len(plan)
    GROUP_END = [sum(t0 < (g + 1) * KB * HG for t0, _ in plan) for g in range(G)]
    unit_of = {t: u for u, (t0, n) in enumerate(plan) for t in range(t0, t0 + n)}

    x_tok = x.rearrange("b t d -> (b t) d")
    out_tok = out.rearrange("b t d -> (b t) d")

    with ExitStack() as ctx:
        def sb(name, shape, dt=F32):
            return ctx.enter_context(nc.sbuf_tensor(name, shape, dt))

        def sem(name):
            return ctx.enter_context(nc.semaphore(name))

        q_dram = nc.dram_tensor("q_split", (NCH * G * P, CH), F16, kind="Internal").ap()
        gate_dram = nc.dram_tensor("q_gates", (NCH * H, CH), F32, kind="Internal").ap()
        rows_dram = nc.dram_tensor("token_rows", (N, RW), F32, kind="Internal").ap()
        slot_dram = nc.dram_tensor("slot_token", (SLOTS, 1), I32, kind="Internal").ap()

        psum = ctx.enter_context(nc.psum_tensor("psum", [P, 8, CH], F32))
        acc = psum[:, 6, :]
        misc = psum[:, 7, :]
        misc16 = misc.bitcast(F16)

        ident = sb("ident", [P, P])
        ident16 = sb("ident16", [P, P], F16)
        upper = sb("upper", [P, P])
        ones = sb("ones", [P, P])
        zero16 = sb("zero16", [P, CH], F16)
        iota_e = sb("iota_e", [P, E])
        iota_m = sb("iota_m", [P, MC])
        iota_t = sb("iota_t", [P, NS])
        iota_p = sb("iota_p", [P, 1])
        warm = sb("warm", [P, 1])
        no_token = sb("no_token", [P, NS], I32)
        tok_step = sb("tok_step", [P, TPC], I32)
        tok_i = sb("tok_i", [P, NCH * TPC], I32)
        gam = sb("gam", [P, 1])
        bet = sb("bet", [P, 1])
        bet_rep = sb("bet_rep", [P, P])
        wqk = sb("wqk", [P, 2, D])
        wqk_g = sb("wqk_g", [P, 2, D])
        wv = sb("wv", [P, D])
        wo = sb("wo", [P, G, D])
        g_heads = sb("g_heads", [P, 2, HD])
        bo = sb("bo", [P, D])
        sw = sb("sw", [P, E])
        swb = sb("swb", [P, E])
        qk_beta = sb("qk_beta", [P, 2, D])

        xres = sb("xres", [P, (NCH + 1) * TPC * D])
        kw = sb("kw", [P, NCH * G * CH], F16)
        vw = sb("vw", [P, NCH * TPC * D])

        st = sb("st", [P, TPC, 6])
        mv = sb("mv", [P, TPC, 2])
        var4 = sb("var4", [P, TPC])
        rs4 = sb("rs4", [P, TPC])
        nt_a = sb("nt_a", [P, 2 * TPC * H])
        nt_b = sb("nt_b", [P, 2 * TPC * H])
        x1 = sb("x1", [P, TPC, D])
        xn = sb("xn", [P, TPC, D])
        x1t = sb("x1t", [P, CH])
        xnt = sb("xnt", [P, CH])
        qk = sb("qk", [P, 2, TPC, D])
        qkn = sb("qkn", [P, 2, TPC, D])
        ss = sb("ss", [P, 2 * TPC * H])
        inv = sb("inv", [P, 2 * TPC * H])
        gsum = sb("gsum", [P, 2 * TPC * H])
        gates = sb("gates", [P, 2, TPC, H])
        qs = sb("qs", [P, TPC * H, 4, HD], F16)
        ks = sb("ks", [P, TPC * H, 4, HD], F16)
        qt = sb("qt", [P, G, CH], F16)
        gate_t = sb("gate_t", [H, CH])

        qm = sb("qm", [P, H, CH], F16)
        gt = sb("gt", [P, G, CH])
        ring = sb("ring", [P, RING, CH])
        ft = sb("ft", [P, G, CH])

        rows = sb("rows", [P, TPC, RW])
        tt = sb("tt", [P, CH])
        lg = sb("lg", [P, TPC, E])
        lmax = sb("lmax", [P, TPC])
        sp_ = sb("sig_pos", [P, TPC, E])
        sn_ = sb("sig_neg", [P, TPC, E])
        ex = sb("ex", [P, TPC, E])
        emax = sb("emax", [P, TPC])
        esum = sb("esum", [P, TPC])
        cand = sb("cand", [P, TPC, E])
        route = sb("route", [P, TPC])
        onehot = sb("onehot", [P, TPC, E])
        rank = sb("rank", [P, 2, TPC, E])
        run = sb("run", [P, E])
        live = sb("live", [P, 1])
        slot_f = sb("slot_f", [P, TPC])
        slot_i = sb("slot_i", [P, TPC], I32)

        grid = sb("grid", [P, E, MC])
        tiles_e = sb("tiles_e", [P, E])
        cum_e = sb("cum_e", [P, E])
        started = sb("started", [P, NS, E])
        began = sb("began", [P, NS, E])
        tile_e = sb("tile_e", [P, NS])
        tile_s = sb("tile_s", [P, NS])
        first_slot = sb("first_slot", [P, NS], I32)
        eid = sb("eid", [P, NS], I32)
        ids = [sb(f"ids{r}", [P, 1], I32) for r in range(IDS_BUFS)]

        ring_flat = ring[:].rearrange("p r n -> p (r n)")
        taken = [0]

        def after_ring(*shape):
            size = 1
            for n in shape:
                size *= n
            at = taken[0]
            taken[0] += size
            assert taken[0] <= RING * CH
            names = "abc"[:len(shape)]
            pattern = f"p ({' '.join(names)}) -> p {' '.join(names)}"
            return ring_flat[:, at:at + size].rearrange(pattern, **dict(zip(names, shape)))

        fr = after_ring(ROWS_BUFS, RW)
        fw1 = after_ring(ROWS_BUFS, F)
        stage = after_ring(ROWS_BUFS, EW)
        fw2 = stage[:, :, 0:FC * D].rearrange("p r (c d) -> p r c d", c=FC)
        fb1 = stage[:, :, FC * D:FC * D + FC]
        fb2 = stage[:, :, FC * D + FC:EW]
        w1_all = kw[:, 0:NCH // B * G * CH].bitcast(F32)
        assert NCH // B * G * CH // 2 >= E * F
        experts = sb("experts", [P, E * EW])
        fo = sb("fo", [P, ROWS_BUFS, D])
        ftt = after_ring(2, P)
        fh = after_ring(2, FC * P)
        fg = after_ring(2, FC * P)

        loaded_x = sem("loaded_x")
        loaded_w = sem("loaded_w")
        const_made = sem("const_made")
        tok_copied = sem("tok_copied")
        wo_cleared = sem("wo_cleared")
        no_token_made = sem("no_token_made")
        pool_turns = sem("pool_turns")
        rows_free = sem("rows_free")
        slots_cleared = sem("slots_cleared")
        weights_made = sem("weights_made")
        misc_full = sem("misc_full")
        misc_free = sem("misc_free")
        vec = sem("vector_step")
        x1_ready = sem("x1_ready")
        xn_ready = sem("xn_ready")
        gsum_ready = sem("gsum_ready")
        gsig_ready = sem("gsig_ready")
        gates_ready = sem("gates_ready")
        qs_ready = sem("qs_ready")
        ks_ready = sem("ks_ready")
        q_stored = sem("q_stored")
        gate_stored = sem("gate_stored")
        q_loaded = [sem(f"q_loaded{g}") for g in range(G)]
        gt_loaded = [sem(f"gt_loaded{g}") for g in range(G)]
        qm_cleared = sem("qm_cleared")
        scores_ready = sem("scores_ready")
        sig_done = sem("sig_done")
        pv_done = sem("pv_done")
        acc_free = sem("acc_free")
        ft_ready = sem("ft_ready")
        t_ready = sem("t_ready")
        d_ready = sem("d_ready")
        esig_ready = sem("esig_ready")
        onehot_ready = sem("onehot_ready")
        row_ready = sem("row_ready")
        rows_stored = sem("rows_stored")
        slots_stored = sem("slots_stored")
        sched_ready = sem("sched_ready")
        ids_loaded = [sem(f"ids_loaded{r}") for r in range(IDS_BUFS)]
        rows_loaded = [sem(f"rows_loaded{r}") for r in range(ROWS_BUFS)]
        experts_loaded = sem("experts_loaded")
        act_turns = sem("act_turns")
        staged = sem("staged")
        rows_cleared = sem("rows_cleared")
        sp_turns = sem("sp_turns")
        turned = sem("rows_turned")
        turned_taken = sem("turned_rows_taken")
        up_done = sem("up_done")
        hidden_ready = sem("hidden_ready")
        gelu_ready = sem("gelu_ready")
        down_done = sem("down_done")
        fo_ready = sem("fo_ready")
        out_stored = [sem(f"out_stored{r}") for r in range(IDS_BUFS)]

        EARLY = QC

        def step_job(b, s):
            done = EARLY * PROLOGUE_JOBS + b * QC * LOOP_JOBS[0]
            return (s - b * QC) * LOOP_JOBS[b] + done

        LAST_POST = EARLY * PROLOGUE_JOBS + QC * (LOOP_JOBS[0] + LOOP_JOBS[1])

        block = ctx.enter_context(nc.Block())

        @block.sync
        def _(sp):
            for c in range(NCH):
                src = x_tok[c * CH:(c + 1) * CH, :].rearrange("(t p) d -> p t d", p=P)
                dst = xres[:, (c + 1) * CH:(c + 2) * CH].rearrange("p (t d) -> p t d", t=TPC)
                sp.dma_start(dst, src).then_inc(loaded_x, 16)

            def store_chunk(c, first_job):
                sp.wait_ge(misc_free, first_job + (J_GATE + 3))
                sp.dma_start(gate_dram[bass.ds(c * H, H), :], gate_t[:]).then_inc(gate_stored, 16)
                sp.wait_ge(misc_free, first_job + (J_Q1 + 3))
                sp.dma_start(q_dram[bass.ds(c * (G * P), G * P), :].rearrange("(g p) n -> p g n", p=P),
                             qt[:]).then_inc(q_stored, 16)

            with sp.Fori(0, EARLY) as c:
                store_chunk(c, c * PROLOGUE_JOBS)

            def load_q(s, g):
                for j in range(HG):
                    sp.dma_start(qm[QR * j:QR * (j + 1), g * HG + j, :],
                                 q_dram[bass.ds(s * (G * P) + (g * P + QR * j), QR), :]).then_inc(q_loaded[g], 16)

            def load_gates(s, g):
                for j in range(HG):
                    sp.dma_start(gt[QR * j:QR * (j + 1), g, :],
                                 gate_dram[bass.ds(s * H + (g * HG + j), 1), :].to_broadcast([QR, CH])
                                 ).then_inc(gt_loaded[g], 16)

            sp.wait_ge(q_stored, 16 * (EARLY + 1))
            sp.wait_ge(gate_stored, 16 * (EARLY + 1))
            sp.wait_ge(qm_cleared, 1)
            for g in range(G):
                load_q(0, g)
                load_gates(0, g)

            by_expert = experts[:].rearrange("p (e n) -> p e n", e=E)
            for e in range(E):
                sp.dma_start(by_expert[:, e, 0:FC * D].rearrange("p (c d) -> p c d", c=FC),
                             w2[e].rearrange("(c p) d -> p c d", p=P)).then_inc(experts_loaded, 16)
                for c in range(FC):
                    sp.dma_start(by_expert[:, e, FC * D + c:FC * D + c + 1],
                                 b1[e, c * P:(c + 1) * P].rearrange("(p a) -> p a", a=1)).then_inc(experts_loaded, 16)
                sp.dma_start(by_expert[:, e, FC * D + FC:EW],
                             b2[e:e + 1, :].to_broadcast([P, D])).then_inc(experts_loaded, 16)

            def load_step(s, g):
                sp.wait_ge(scores_ready, s * U + (GROUP_END[g] - U))
                load_q(s, g)
                sp.wait_ge(acc_free, s * G + (g + 2 - G))
                load_gates(s, g)

            with sp.Fori(1, QC + 1) as s:
                sp.wait_ge(q_stored, s * 16 + 32)
                sp.wait_ge(gate_stored, s * 16 + 32)
                for g in range(G - 1):
                    load_step(s, g)
                store_chunk(s + (QC - 1), step_job(0, s - 1) + POST_JOBS)
                load_step(s, G - 1)
            for e in range(E):
                sp.dma_start(w1_all[:, e * F:(e + 1) * F], w1[e]).then_inc(experts_loaded, 16)
            with sp.Fori(QC + 1, NCH) as s:
                sp.wait_ge(q_stored, s * 16 + 32)
                sp.wait_ge(gate_stored, s * 16 + 32)
                for g in range(G):
                    load_step(s, g)
            sp.wait_ge(scores_ready, (NCH - 1) * U + GROUP_END[0])
            load_q(NCH - 1, 0)

            def wait(sem_, value):
                sp.wait_ge(sem_, value)
                sp.sem_inc(sp_turns, 1)

            def fetch(base, r):
                x = base + r
                wait(out_stored[r], base * (16 // IDS_BUFS) + 16)
                slot = sp.value_load(first_slot[0:1, bass.ds(x, 1)], min_val=0, max_val=SLOTS - P)
                sp.dma_start(ids[r][:], slot_dram[bass.ds(slot, P), :]).then_inc(ids_loaded[r], 16)

            sp.wait_ge(sched_ready, 1)
            with sp.Fori(0, NT // IDS_BUFS) as rnd:
                for r in range(IDS_BUFS):
                    fetch(rnd * IDS_BUFS, r)
            for r in range(AHEAD):
                fetch(NT, r)
        @block.gpsimd
        def _(pool):
            made = [0]

            def make(ins):
                made[0] += 1
                ins.then_inc(const_made, 1)

            make(pool.memset(ident[:], 0.0))
            make(pool.memset(ident16[:], 0.0))
            make(pool.memset(upper[:], 0.0))
            pool.wait_ge(const_made, made[0])
            for m in (ident, ident16):
                make(pool.affine_select(out=m[:], in_=m[:], compare_op=ALU.not_equal, fill=1.0, base=0,
                                        pattern=[[-1, P]], channel_multiplier=1))
            make(pool.affine_select(out=upper[:], in_=upper[:], compare_op=ALU.is_ge, fill=1.0, base=0,
                                    pattern=[[-1, P]], channel_multiplier=1))
            make(pool.memset(ones[:], 1.0))
            make(pool.memset(zero16[:], 0.0))
            make(pool.iota(iota_e[:], pattern=[[1, E]], base=0, channel_multiplier=0,
                           allow_small_or_imprecise_dtypes=True))
            make(pool.iota(iota_m[:], pattern=[[P, MC]], base=0, channel_multiplier=0,
                           allow_small_or_imprecise_dtypes=True))
            make(pool.iota(iota_t[:], pattern=[[1, NS]], base=0, channel_multiplier=0,
                           allow_small_or_imprecise_dtypes=True))
            make(pool.iota(iota_p[:], pattern=[[0, 1]], base=0, channel_multiplier=1,
                           allow_small_or_imprecise_dtypes=True))
            make(pool.iota(tok_i[:], pattern=[[P, NCH * TPC]], base=0, channel_multiplier=1))
            make(pool.memset(xres[:, 0:CH], 0.0))
            make(pool.memset(ft[:], 0.0))
            make(pool.memset(run[:], 0.0))
            make(pool.memset(live[:], 0.0))
            make(pool.memset(rows[:], 0.0))
            assert made[0] == CONSTS
            pool.memset(qm[:], 0.0).then_inc(qm_cleared, 1)
            pool.memset(no_token[:], N).then_inc(no_token_made, 1)
            pool.wait_ge(no_token_made, 1)
            for i in range(0, SLOTS // P, NS):
                n = min(NS, SLOTS // P - i)
                pool.dma_start(slot_dram[i * P:(i + n) * P, :].rearrange("(p n) c -> p (n c)", p=P),
                               no_token[:, 0:n]).then_inc(slots_cleared, 16)
            pool.wait_ge(slots_cleared, 16 * len(range(0, SLOTS // P, NS)))

            def wait(sem_, value):
                pool.wait_ge(sem_, value)
                pool.sem_inc(pool_turns, 1)

            with pool.Fori(0, NCH) as c:
                wait(row_ready, c + 2)
                pool.tensor_copy(tok_step[:], tok_i[:, bass.ds(c * TPC, TPC)]).then_inc(tok_copied, 1)
                wait(tok_copied, c + 1)
                pool.dma_start(rows_dram[bass.ds(c * CH, CH), :].rearrange("(t p) w -> p t w", p=P),
                               rows[:]).then_inc(rows_stored, 16)
                for t in range(TPC):
                    pool.indirect_dma_start(slot_dram[:, :], bass.IndirectOffsetOnAxis(ap=slot_i[:, t:t + 1], axis=0),
                                            tok_step[:, t:t + 1], None).then_inc(slots_stored, 16)
                wait(rows_stored, c * 16 + 16)
                wait(slots_stored, c * (16 * TPC) + 16 * TPC)
                pool.sem_inc(rows_free, 1)

            pool.wait_ge(acc_free, NCH * G + 1)
            pool.memset(fr, 0.0).then_inc(rows_cleared, 1)
            for r in range(IDS_BUFS):
                pool.memset(ids[r][:], N).then_inc(rows_cleared, 1)
            pool.memset(fo[:], 0.0).then_inc(rows_cleared, 1)
            pool.wait_ge(rows_cleared, 2 + IDS_BUFS)

            def gather(base, r):
                wait(ids_loaded[r % IDS_BUFS], base * (16 // IDS_BUFS) + 16 * (r // IDS_BUFS + 1))
                pool.indirect_dma_start(fr[:, r % ROWS_BUFS, :], None, rows_dram[:, :],
                                        bass.IndirectOffsetOnAxis(ap=ids[r % IDS_BUFS][:], axis=0),
                                        bounds_check=N - 1, oob_is_err=False).then_inc(rows_loaded[r % ROWS_BUFS], 16)

            def scatter(r):
                pool.indirect_dma_start(out_tok[:, :], bass.IndirectOffsetOnAxis(ap=ids[r][:], axis=0),
                                        fo[:, r % ROWS_BUFS, :], None,
                                        bounds_check=N - 1, oob_is_err=False).then_inc(out_stored[r], 16)

            for r in range(IDS_BUFS):
                scatter(r)
            for r in range(AHEAD):
                gather(0, r)
            with pool.Fori(0, NT // IDS_BUFS) as rnd:
                for r in range(IDS_BUFS):
                    gather(rnd * IDS_BUFS, r + AHEAD)
                    wait(fo_ready, rnd * IDS_BUFS + (r + 1 + ROWS_BUFS))
                    scatter(r)
            for r in range(IDS_BUFS):
                wait(out_stored[r], 16 * (NT + IDS_BUFS) // IDS_BUFS)

        @block.scalar
        def _(act):
            act.dma_start(gam[:], gamma.rearrange("(p a) -> p a", a=1)).then_inc(loaded_w, 16)
            act.dma_start(bet[:], beta.rearrange("(p a) -> p a", a=1)).then_inc(loaded_w, 16)
            act.dma_start(wqk[:, 0, :], w_q).then_inc(loaded_w, 16)
            act.dma_start(wqk[:, 1, :], w_k).then_inc(loaded_w, 16)
            act.dma_start(wv[:], w_v).then_inc(loaded_w, 16)
            act.dma_start(g_heads[:, 0, :], g_q.rearrange("(a d) -> a d", a=1).to_broadcast([P, HD])).then_inc(loaded_w, 16)
            act.dma_start(g_heads[:, 1, :], g_k.rearrange("(a d) -> a d", a=1).to_broadcast([P, HD])).then_inc(loaded_w, 16)
            act.dma_start(bo[:], b_o.rearrange("(a d) -> a d", a=1).to_broadcast([P, D])).then_inc(loaded_w, 16)
            act.dma_start(sw[:], switch_w).then_inc(loaded_w, 16)
            act.dma_start(swb[:], switch_b.rearrange("(a d) -> a d", a=1).to_broadcast([P, E])).then_inc(loaded_w, 16)
            act.wait_ge(wo_cleared, 1)
            wo_heads = w_o.rearrange("(g j d) n -> j d g n", j=HG, d=HD)
            for j in range(HG):
                act.dma_start(wo[QR * j:QR * j + HD, :, :], wo_heads[j]).then_inc(loaded_w, 16)

            with act.Fori(0, EARLY) as c:
                act.wait_ge(gsum_ready, c + 1)
                act.activation(gsum[:], gsum[:], ACT.Sigmoid).then_inc(gsig_ready, 1)

            def units(s, lo, hi):
                for u in range(lo, hi):
                    t0, n = plan[u]
                    act.wait_ge(scores_ready, s * U + (u + 1))
                    kb_last = (t0 + n - 1 - RING) // HG
                    act.wait_ge(pv_done, s * (G * KB) + (kb_last + 1 + G * KB))
                    r0, b0 = t0 % RING, u % BANKS * UNIT
                    act.activation(ring[:, r0:r0 + n, :], psum[:, b0:b0 + n, :], ACT.Sigmoid,
                               scale=SHARP / SPLIT ** 2, bias=-SHARP * THRESHOLD).then_inc(sig_done, 1)

            for b in range(B):
                with act.Fori(b * QC, (b + 1) * QC) as s:
                    units(s, 0, ROUTES_AT)
                    act.wait_ge(d_ready, s + 1)
                    act.activation(sp_[:], lg[:], ACT.Sigmoid)
                    act.activation(sn_[:], lg[:], ACT.Sigmoid, scale=-1.0).then_inc(esig_ready, 1)
                    units(s, ROUTES_AT, GATES_AT)
                    if b + 1 < B:
                        act.wait_ge(gsum_ready, s + (EARLY + 1))
                        act.activation(gsum[:], gsum[:], ACT.Sigmoid).then_inc(gsig_ready, 1)
                    units(s, GATES_AT, U)
            act.wait_ge(d_ready, NCH + 1)
            act.activation(sp_[:], lg[:], ACT.Sigmoid)
            act.activation(sn_[:], lg[:], ACT.Sigmoid, scale=-1.0).then_inc(esig_ready, 1)

            def stage_weights(x, r):
                act.wait_ge(fo_ready, x + 1)
                act.sem_inc(act_turns, 1)
                e = act.value_load(eid[0:1, bass.ds(x, 1)], min_val=0, max_val=E - 1)
                act.activation(fw1[:, r, :], w1_all[:, bass.ds(e * F, F)], ACT.Copy)
                act.activation(stage[:, r, :], experts[:, bass.ds(e * EW, EW)], ACT.Copy).then_inc(staged, 1)

            act.activation(warm[:], iota_p[:], ACT.Gelu_apprx_tanh)
            act.wait_ge(experts_loaded, 16 * E * (FC + 3))
            act.wait_ge(sched_ready, 1)
            for r in range(2):
                stage_weights(r, r)
            with act.Fori(0, NT // ROWS_BUFS) as rnd:
                for r in range(ROWS_BUFS):
                    x = rnd * ROWS_BUFS + r
                    act.wait_ge(hidden_ready, x + 3)
                    act.wait_ge(down_done, x + 1)
                    act.activation(fg[:, r % 2, :], fh[:, r % 2, :], ACT.Gelu_apprx_tanh).then_inc(gelu_ready, 1)
                    stage_weights(x + 2, (r + 2) % ROWS_BUFS)

        @block.vector
        def _(dve):
            steps = [0]

            def link(ins, base=0):
                steps[0] += 1
                ins.then_inc(vec, 1)
                dve.wait_ge(vec, base + steps[0])

            def rsqrt(y, a, t, u, base):
                link(dve.tensor_scalar(t.bitcast(I32), a.bitcast(I32), 1, None, ALU.logical_shift_right), base)
                link(dve.tensor_scalar(y.bitcast(I32), t.bitcast(I32), -1.0, float(RSQRT_SEED), ALU.mult, ALU.add), base)
                for _ in range(3):
                    link(dve.scalar_tensor_tensor(t, y, -0.5, y, ALU.mult, ALU.mult), base)
                    link(dve.tensor_tensor(u, t, a, ALU.mult), base)
                    link(dve.scalar_tensor_tensor(y, u, 1.5, y, ALU.add, ALU.mult), base)

            def layernorm(dst, src, base, done=None):
                for t in range(TPC):
                    last = dve.bn_stats(st[:, t, :], src[:, t, :])
                link(last, base)
                m_e, m_o, v_e, v_o = st[:, :, 1], st[:, :, 4], st[:, :, 2], st[:, :, 5]
                dve.tensor_tensor(mv[:, :, 0], m_e, m_o, ALU.add)
                dve.tensor_tensor(mv[:, :, 1], m_e, m_o, ALU.subtract)
                link(dve.tensor_tensor(var4[:], v_e, v_o, ALU.add), base)
                dve.tensor_scalar(mv[:, :, 0], mv[:, :, 0], 0.5, None, ALU.mult)
                dve.scalar_tensor_tensor(mv[:, :, 1], mv[:, :, 1], 0.25, mv[:, :, 1], ALU.mult, ALU.mult)
                link(dve.tensor_scalar(var4[:], var4[:], 1.0 / D, LN_EPS, ALU.mult, ALU.add), base)
                link(dve.tensor_tensor(var4[:], var4[:], mv[:, :, 1], ALU.add), base)
                rsqrt(rs4[:], var4[:], nt_a[:, 0:TPC], nt_b[:, 0:TPC], base)
                for t in range(TPC):
                    last = dve.tensor_scalar(dst[:, t, :], src[:, t, :], mv[:, t, 0:1], rs4[:, t:t + 1],
                                             ALU.subtract, ALU.mult)
                return last

            dve.sem_inc(misc_free, 1)
            dve.sem_inc(acc_free, 1)
            dve.sem_inc(pv_done, G * KB)
            dve.sem_inc(q_stored, 16)
            dve.sem_inc(gate_stored, 16)
            dve.sem_inc(rows_free, 2)
            dve.sem_inc(fo_ready, ROWS_BUFS)
            for s_ in (turned_taken, up_done, hidden_ready, gelu_ready, down_done):
                dve.sem_inc(s_, 2)
            dve.memset(wo[:], 0.0).then_inc(wo_cleared, 1)
            dve.wait_ge(loaded_w, 16 * WEIGHT_LOADS)
            dve.wait_ge(const_made, CONSTS)
            dve.tensor_scalar(bet_rep[:], ones[:], bet[:], None, ALU.mult)
            dve.tensor_scalar(wqk_g[:].rearrange("p a d -> p (a d)"), wqk[:].rearrange("p a d -> p (a d)"), gam[:],
                              None, ALU.mult).then_inc(weights_made, 1)
            dve.wait_ge(misc_full, 1)
            dve.tensor_copy(qk_beta[:].rearrange("p a d -> p (a d)"), misc[:, 0:2 * D]).then_inc(misc_free, 1)
            dve.wait_ge(misc_free, 2)
            dve.wait_ge(loaded_x, 16 * NCH)

            def prologue_parts(c, base, first_job):
                return (lambda: front(c, base, first_job)), (lambda: back(c, base, first_job))

            def front(c, base, first_job):
                job = lambda j: first_job + (j + 2)
                xc = xres[:, bass.ds(c * CH + CH, CH)].rearrange("p (t d) -> p t d", t=TPC)
                layernorm(x1, xc, base).then_inc(x1_ready, 1)
                dve.wait_ge(x1_ready, c + 1)
                layernorm(xn, x1, base).then_inc(xn_ready, 1)
                dve.wait_ge(misc_full, job(J_X1T))
                dve.tensor_copy(x1t[:], misc).then_inc(misc_free, 1)
                dve.wait_ge(misc_full, job(J_XNT))
                dve.tensor_copy(xnt[:], misc).then_inc(misc_free, 1)
                for half, j in ((0, J_QK0), (1, J_QK1)):
                    dve.wait_ge(misc_full, job(j))
                    dve.tensor_tensor(qk[:, :, 2 * half:2 * half + 2, :].rearrange("p a t d -> p t a d"),
                                      misc.rearrange("p (t a d) -> p t a d", t=2, a=2),
                                      qk_beta[:].unsqueeze(1).to_broadcast([P, 2, 2, D]),
                                      ALU.add).then_inc(misc_free, 1)
                dve.wait_ge(misc_free, job(J_QK1) + 1)
                qk_h = qk[:].rearrange("p a t (h d) -> p (a t h) d", d=HD)
                qkn_h = qkn[:].rearrange("p a t (h d) -> p (a t h) d", d=HD)
                link(dve.tensor_tensor(qkn_h, qk_h, qk_h, ALU.mult), base)
                link(dve.tensor_reduce(ss[:], qkn_h, AX.X, ALU.add), base)
                link(dve.tensor_scalar(ss[:], ss[:], NORM_EPS2, None, ALU.max), base)
                rsqrt(inv[:], ss[:], nt_a[:], nt_b[:], base)

            def back(c, base, first_job):
                job = lambda j: first_job + (j + 2)
                NH = 2 * TPC * H
                qk_h = qk[:].rearrange("p a t (h d) -> p (a t h) d", d=HD)
                qkn_h = qkn[:].rearrange("p a t (h d) -> p (a t h) d", d=HD)
                link(dve.tensor_tensor(qkn_h, qk_h, inv[:].unsqueeze(2).to_broadcast([P, NH, HD]), ALU.mult), base)
                for a in range(2):
                    last = dve.tensor_tensor(qk[:, a].rearrange("p t (h d) -> p (t h) d", d=HD),
                                             qkn[:, a].rearrange("p t (h d) -> p (t h) d", d=HD),
                                             g_heads[:, a, :].unsqueeze(1).to_broadcast([P, TPC * H, HD]), ALU.mult)
                link(last, base)
                dve.tensor_reduce(gsum[:], qk_h, AX.X, ALU.add).then_inc(gsum_ready, 1)
                q3 = qkn[:, 0].rearrange("p t (h d) -> p (t h) d", d=HD)
                k3 = qkn[:, 1].rearrange("p t (h d) -> p (t h) d", d=HD)
                for i in (0, 1):
                    dve.tensor_scalar(qs[:, :, i, :], q3, SPLIT, None, ALU.mult)
                for i in (0, 2):
                    last = dve.tensor_scalar(ks[:, :, i, :], k3, SPLIT, None, ALU.mult)
                link(last, base)
                dve.scalar_tensor_tensor(qs[:, :, 2, :], q3, SPLIT, qs[:, :, 0, :], ALU.mult, ALU.subtract)
                link(dve.scalar_tensor_tensor(ks[:, :, 1, :], k3, SPLIT, ks[:, :, 0, :], ALU.mult, ALU.subtract), base)
                dve.tensor_copy(qs[:, :, 3, :], qs[:, :, 2, :]).then_inc(qs_ready, 1)
                dve.tensor_copy(ks[:, :, 3, :], ks[:, :, 1, :]).then_inc(ks_ready, 1)
                dve.wait_ge(gsig_ready, c + 1)
                dve.tensor_scalar(gates[:].rearrange("p a t h -> p (a t h)"), gsum[:], 0.75, 0.25,
                                  ALU.mult, ALU.add).then_inc(gates_ready, 1)
                dve.wait_ge(gates_ready, c + 1)
                dve.wait_ge(misc_full, job(J_V))
                dve.tensor_tensor(vw[:, bass.ds(c * CH, CH)].rearrange("p (n d) -> p n d", d=HD),
                                  misc.rearrange("p (n d) -> p n d", d=HD),
                                  gates[:, 1].rearrange("p t h -> p (t h)").unsqueeze(2).to_broadcast([P, TPC * H, HD]),
                                  ALU.mult).then_inc(misc_free, 1)
                dve.wait_ge(misc_full, job(J_GATE))
                dve.wait_ge(gate_stored, c * 16 + 16)
                dve.tensor_copy(gate_t[:], misc[0:H, :]).then_inc(misc_free, 1)
                for half, j in ((0, J_Q0), (1, J_Q1)):
                    dve.wait_ge(misc_full, job(j))
                    if half == 0:
                        dve.wait_ge(q_stored, c * 16 + 16)
                    dve.tensor_copy(qt[:, :, 2 * P * half:2 * P * (half + 1)].rearrange("p g (t n) -> p t g n", t=2),
                                    misc16.rearrange("p (t g n) -> p t g n", t=2, g=G)).then_inc(misc_free, 1)
                kc = kw[:, bass.ds(c * (G * CH), G * CH)].rearrange("p (g n) -> p g n", g=G)
                for half, j in ((0, J_K0), (1, J_K1)):
                    dve.wait_ge(misc_full, job(j))
                    dve.tensor_copy(kc[:, :, 2 * P * half:2 * P * (half + 1)].rearrange("p g (t n) -> p t g n", t=2),
                                    misc16.rearrange("p (t g n) -> p t g n", t=2, g=G)).then_inc(misc_free, 1)

            with dve.Fori(0, EARLY) as c:
                for part in prologue_parts(c, c * PROLOGUE_STEPS, c * PROLOGUE_JOBS):
                    part()
                assert steps[0] == PROLOGUE_STEPS, steps[0]
            base0 = (EARLY - 1) * PROLOGUE_STEPS

            def take_group(s, g):
                dve.wait_ge(gt_loaded[g], s * (16 * HG) + 16 * HG)
                dve.wait_ge(pv_done, s * (G * KB) + (G * KB + KB * (g + 1)))
                dve.tensor_tensor(ft[:, g, :], acc, gt[:, g, :], ALU.mult).then_inc(acc_free, 1)

            def post_parts(s, base, first_job):
                job = lambda j: first_job + (j + 2)
                x2 = rows[:, :, D:2 * D]
                tn = rows[:, :, 0:D]
                xc = xres[:, bass.ds(s * CH, CH)].rearrange("p (t d) -> p t d", t=TPC)

                def residual():
                    dve.wait_ge(misc_full, job(J_WO))
                    dve.wait_ge(rows_free, s + 1)
                    dve.tensor_tensor(x2, misc.rearrange("p (t d) -> p t d", t=TPC),
                                      bo[:].unsqueeze(1).to_broadcast([P, TPC, D]), ALU.add).then_inc(misc_free, 1)
                    dve.wait_ge(misc_free, job(J_WO) + 1)
                    link(dve.tensor_tensor(x2, x2, xc, ALU.add), base)
                    layernorm(tn, x2, base).then_inc(t_ready, 1)

                def logits():
                    dve.wait_ge(misc_full, job(J_LNT))
                    dve.tensor_copy(tt[:], misc).then_inc(misc_free, 1)
                    dve.wait_ge(misc_full, job(J_LOGITS))
                    dve.tensor_tensor(lg[:], misc[:, 0:TPC * E].rearrange("p (t e) -> p t e", e=E),
                                      swb[:].unsqueeze(1).to_broadcast([P, TPC, E]), ALU.add).then_inc(misc_free, 1)
                    dve.wait_ge(misc_free, job(J_LOGITS) + 1)
                    link(dve.tensor_reduce(lmax[:], lg[:], AX.X, ALU.max), base)
                    dve.tensor_tensor(lg[:], lg[:], lmax[:].unsqueeze(2).to_broadcast([P, TPC, E]),
                                      ALU.subtract).then_inc(d_ready, 1)

                def routes():
                    dve.wait_ge(esig_ready, s + 1)
                    link(dve.reciprocal(sn_[:], sn_[:]), base)
                    link(dve.tensor_tensor(ex[:], sp_[:], sn_[:], ALU.mult), base)
                    dve.tensor_reduce(esum[:], ex[:], AX.X, ALU.add)
                    link(dve.tensor_reduce(emax[:], ex[:], AX.X, ALU.max), base)
                    dve.tensor_tensor(cand[:], ex[:], emax[:].unsqueeze(2).to_broadcast([P, TPC, E]), ALU.is_ge)
                    link(dve.reciprocal(esum[:], esum[:]), base)
                    dve.tensor_tensor(rows[:, :, 2 * D:RW], emax[:].unsqueeze(2), esum[:].unsqueeze(2), ALU.mult)
                    link(dve.scalar_tensor_tensor(cand[:], cand[:], -float(E),
                                                  iota_e[:].unsqueeze(1).to_broadcast([P, TPC, E]),
                                                  ALU.mult, ALU.add), base)
                    link(dve.tensor_reduce(route[:], cand[:], AX.X, ALU.min), base)
                    link(dve.tensor_scalar(route[:], route[:], float(E), None, ALU.add), base)
                    dve.tensor_tensor(onehot[:], iota_e[:].unsqueeze(1).to_broadcast([P, TPC, E]),
                                      route[:].unsqueeze(2).to_broadcast([P, TPC, E]),
                                      ALU.is_equal).then_inc(onehot_ready, 1)
                    dve.wait_ge(onehot_ready, s + 1)

                def ranks():
                    dve.wait_ge(misc_full, job(J_RANK))
                    dve.tensor_copy(rank[:].rearrange("p a t e -> p (a t e)"),
                                    misc[:, 0:2 * TPC * E]).then_inc(misc_free, 1)
                    dve.wait_ge(misc_free, job(J_RANK) + 1)
                    for t in range(TPC):
                        dve.tensor_tensor(rank[:, 0, t, :], rank[:, 0, t, :], run[:], ALU.add)
                        link(dve.tensor_tensor(run[:], run[:], rank[:, 1, t, :], ALU.add), base)
                    link(dve.tensor_tensor(rank[:, 0], rank[:, 0], onehot[:], ALU.mult), base)
                    link(dve.tensor_reduce(slot_f[:], rank[:, 0], AX.X, ALU.add), base)
                    dve.tensor_scalar(run[:], run[:], live[:], None, ALU.mult)
                    link(dve.scalar_tensor_tensor(slot_f[:], route[:], float(CAP), slot_f[:], ALU.mult, ALU.add), base)
                    dve.memset(live[:], 1.0)
                    dve.tensor_copy(slot_i[:], slot_f[:]).then_inc(row_ready, 1)
                    dve.wait_ge(row_ready, s + 1)

                return residual, logits, routes, ranks

            for b in range(B):
                with dve.Fori(b * QC, (b + 1) * QC) as s:
                    n0 = steps[0]
                    base = (s - b * QC) * LOOP_STEPS[b] + base0
                    residual, logits, routes, ranks = post_parts(s, base, step_job(b, s))
                    residual()
                    logits()
                    routes()
                    take_group(s, 0)
                    ranks()
                    if b + 1 < B:
                        make, finish = prologue_parts(s + EARLY, base, step_job(b, s) + POST_JOBS)
                        make()
                        take_group(s, 1)
                        finish()
                    else:
                        take_group(s, 1)
                    take_group(s, 2)
                    take_group(s, 3)
                    assert steps[0] - n0 == LOOP_STEPS[b], steps[0] - n0
                base0 += (QC - 1) * LOOP_STEPS[b]
            for part in post_parts(NCH, base0, LAST_POST):
                part()

            b3 = lambda ap, shape, at: ap.unsqueeze(at).to_broadcast(shape)
            link(dve.tensor_tensor(grid[:], b3(run[:], [P, E, MC], 2), b3(iota_m[:], [P, E, MC], 1), ALU.is_gt), base0)
            link(dve.tensor_reduce(tiles_e[:], grid[:], AX.X, ALU.add), base0)
            link(dve.tensor_copy(cum_e[:], tiles_e[:]), base0)
            for e in range(1, E):
                link(dve.tensor_tensor(cum_e[:, e:e + 1], cum_e[:, e - 1:e], tiles_e[:, e:e + 1], ALU.add), base0)
            link(dve.tensor_tensor(started[:], b3(cum_e[:], [P, NS, E], 1), b3(iota_t[:], [P, NS, E], 2), ALU.is_le), base0)
            dve.tensor_reduce(tile_e[:], started[:], AX.X, ALU.add)
            link(dve.tensor_tensor(began[:], started[:], b3(tiles_e[:], [P, NS, E], 1), ALU.mult), base0)
            link(dve.tensor_reduce(tile_s[:], began[:], AX.X, ALU.add), base0)
            link(dve.tensor_tensor(tile_s[:], iota_t[:], tile_s[:], ALU.subtract), base0)
            link(dve.tensor_scalar(tile_s[:], tile_s[:], float(P), None, ALU.mult), base0)
            link(dve.scalar_tensor_tensor(tile_s[:], tile_e[:], float(CAP), tile_s[:], ALU.mult, ALU.add), base0)
            dve.tensor_copy(first_slot[:], tile_s[:])
            dve.tensor_scalar(eid[:], tile_e[:], float(E - 1), None, ALU.min).then_inc(sched_ready, 1)

            def add_b1(base, r):
                x = base + r
                r4 = r % ROWS_BUFS
                dve.wait_ge(up_done, x + 3)
                dve.wait_ge(staged, x + 1)
                dve.wait_ge(gelu_ready, x + 1)
                dve.tensor_tensor(fh[:, r % 2, :].rearrange("p (c n) -> p c n", c=FC),
                                  psum[:, 2 + r % 2, :].rearrange("p (c n) -> p c n", c=FC),
                                  fb1[:, r4, :].unsqueeze(2).to_broadcast([P, FC, P]), ALU.add).then_inc(hidden_ready, 1)

            def take_turned(base, r):
                x = base + r
                dve.wait_ge(turned, x + 1)
                dve.wait_ge(up_done, x + 1)
                dve.tensor_copy(ftt[:, r % 2, :], psum[:, r % 2, 0:P]).then_inc(turned_taken, 1)

            FFN_STEPS = IDS_BUFS
            take_turned(0, 0)
            take_turned(0, 1)
            add_b1(0, 0)
            with dve.Fori(0, NT // IDS_BUFS) as rnd:
                x8 = rnd * IDS_BUFS
                n0 = steps[0]
                base = rnd * FFN_STEPS + base0
                for r in range(IDS_BUFS):
                    r4 = r % ROWS_BUFS
                    add_b1(x8, r + 1)
                    take_turned(x8, r + 2)
                    dve.wait_ge(down_done, x8 + (r + 3))
                    dve.wait_ge(rows_loaded[r4], x8 * (16 // ROWS_BUFS) + 16 * (r // ROWS_BUFS + 1))
                    dve.wait_ge(out_stored[(r + ROWS_BUFS) % IDS_BUFS], rnd * 16 + (16 if r < ROWS_BUFS else 32))
                    link(dve.tensor_tensor(fo[:, r4, :], psum[:, 4 + r % 2, 0:D], fb2[:, r4, :], ALU.add), base)
                    dve.scalar_tensor_tensor(fo[:, r4, :], fo[:, r4, :], fr[:, r4, 2 * D:RW], fr[:, r4, D:2 * D],
                                             ALU.mult, ALU.add).then_inc(fo_ready, 1)
                assert steps[0] - n0 == FFN_STEPS, steps[0] - n0

        @block.tensor
        def _(pe):
            pe.wait_ge(const_made, CONSTS)
            pe.matmul(acc, zero16[:, 0:P], zero16[:], start=True, stop=True)
            pe.wait_ge(weights_made, 1)
            pe.wait_ge(misc_free, 1)
            pe.matmul(misc[:, 0:2 * D], bet_rep[:], wqk[:].rearrange("p a d -> p (a d)"),
                      start=True, stop=True).then_inc(misc_full, 1)

            def prologue_jobs(c, first_job):
                def free(j):
                    pe.wait_ge(misc_free, first_job + (j + 2))

                def turn_x1():
                    pe.wait_ge(x1_ready, c + 1)
                    free(J_X1T)
                    for t in range(TPC):
                        last = pe.transpose(misc[:, t * P:(t + 1) * P], x1[:, t, :], ident[:])
                    last.then_inc(misc_full, 1)

                def turn_xn():
                    pe.wait_ge(xn_ready, c + 1)
                    free(J_XNT)
                    for t in range(TPC):
                        last = pe.transpose(misc[:, t * P:(t + 1) * P], xn[:, t, :], ident[:])
                    last.then_inc(misc_full, 1)

                def make_qk(half):
                    free((J_QK0, J_QK1)[half])
                    for t in range(2):
                        tile = 2 * half + t
                        last = pe.matmul(misc[:, t * 2 * D:(t + 1) * 2 * D], xnt[:, tile * P:(tile + 1) * P],
                                         wqk_g[:].rearrange("p a d -> p (a d)"), start=True, stop=True)
                    last.then_inc(misc_full, 1)

                def make_v():
                    free(J_V)
                    for t in range(TPC):
                        last = pe.matmul(misc[:, t * D:(t + 1) * D], x1t[:, t * P:(t + 1) * P], wv[:],
                                         start=True, stop=True)
                    last.then_inc(misc_full, 1)

                def turn_gates():
                    pe.wait_ge(gates_ready, c + 1)
                    free(J_GATE)
                    for t in range(TPC):
                        last = pe.transpose(misc[0:H, t * P:(t + 1) * P], gates[:, 0, t, :], ident[:])
                    last.then_inc(misc_full, 1)

                def turn_split(src, made, j, half):
                    pe.wait_ge(made, c + 1)
                    free(j)
                    for t in range(2):
                        for g in range(G):
                            r0 = (2 * half + t) * H + g * HG
                            at = (t * G + g) * P
                            last = pe.transpose(misc16[:, at:at + P],
                                                src[:, r0:r0 + HG, :, :].rearrange("p h c d -> p (h c d)"),
                                                ident16[:])
                    last.then_inc(misc_full, 1)

                return (turn_x1, turn_xn, lambda: make_qk(0), lambda: make_qk(1), make_v, turn_gates,
                        lambda: turn_split(qs, qs_ready, J_Q0, 0), lambda: turn_split(qs, qs_ready, J_Q1, 1),
                        lambda: turn_split(ks, ks_ready, J_K0, 0), lambda: turn_split(ks, ks_ready, J_K1, 1))

            with pe.Fori(0, EARLY) as c:
                for job in prologue_jobs(c, c * PROLOGUE_JOBS):
                    job()
            pe.wait_ge(misc_free, EARLY * PROLOGUE_JOBS + 2)

            def scores(b, s, u):
                over, v = divmod(u, U)
                t0, n = plan[v]
                if s is not None:
                    pe.wait_ge(sig_done, s * U + (u - BANKS + 1))
                for i in range(n):
                    g, kb, j = (t0 + i) // (KB * HG), (t0 + i) // HG % KB, (t0 + i) % HG
                    if (t0 + i) % (KB * HG) == 0:
                        first = 16 * HG * (1 + over)
                        pe.wait_ge(q_loaded[g], first if s is None else s * (16 * HG) + first)
                    at = ((b * QC + kb // TPC) * G + g) * CH + kb % TPC * P
                    keys = kw[:, at:at + P]
                    if over and b + 1 < B:
                        keys = kw[:, bass.ds((s + 1) // QC * (QC * G * CH) + at, P)]
                    last = pe.matmul(psum[:, u % BANKS * UNIT + i, :], keys, qm[:, g * HG + j, :],
                                     start=True, stop=True)
                last.then_inc(scores_ready, 1)

            def values(b, s, g, kb):
                pe.wait_ge(sig_done, s * U + (unit_of[(g * KB + kb) * HG + HG - 1] + 1))
                if kb == 0:
                    pe.wait_ge(acc_free, s * G + (g + 1))
                for j in range(HG):
                    tile = (g * KB + kb) * HG + j
                    at = (b * KB + kb) * D + (g * HG + j) * HD
                    last = pe.matmul(acc[QR * j:QR * j + HD, :], vw[:, at:at + HD],
                                     ring[:, tile % RING, :],
                                     start=(kb == 0), stop=(kb == KB - 1), tile_position=(0, QR * j))
                last.then_inc(pv_done, 1)

            def post_jobs(s, first_job):
                def free(j):
                    pe.wait_ge(misc_free, first_job + (j + 2))

                def project():
                    free(J_WO)
                    for t in range(TPC):
                        for g in range(G):
                            last = pe.matmul(misc[:, t * D:(t + 1) * D], ft[:, g, t * P:(t + 1) * P], wo[:, g, :],
                                             start=(g == 0), stop=(g == G - 1))
                    last.then_inc(misc_full, 1)

                def turn():
                    pe.wait_ge(t_ready, s + 1)
                    free(J_LNT)
                    for t in range(TPC):
                        last = pe.transpose(misc[:, t * P:(t + 1) * P], rows[:, t, 0:D], ident[:])
                    last.then_inc(misc_full, 1)

                def route():
                    free(J_LOGITS)
                    for t in range(TPC):
                        last = pe.matmul(misc[:, t * E:(t + 1) * E], tt[:, t * P:(t + 1) * P], sw[:],
                                         start=True, stop=True)
                    last.then_inc(misc_full, 1)

                def count():
                    pe.wait_ge(onehot_ready, s + 1)
                    free(J_RANK)
                    oh = onehot[:].rearrange("p t e -> p (t e)")
                    pe.matmul(misc[:, 0:TPC * E], upper[:], oh, start=True, stop=True)
                    pe.matmul(misc[:, TPC * E:2 * TPC * E], ones[:], oh, start=True, stop=True).then_inc(misc_full, 1)

                return project, turn, route, count

            for u in range(BANKS):
                scores(0, None, u)
            for b in range(B):
                with pe.Fori(b * QC, (b + 1) * QC) as s:
                    jobs = dict(zip(POST_AT, post_jobs(s, step_job(b, s))))
                    if b + 1 < B:
                        jobs.update(zip(PROLOGUE_AT, prologue_jobs(s + EARLY, step_job(b, s) + POST_JOBS)))
                    for u in range(U):
                        if u == U - BANKS:
                            pe.wait_ge(misc_free, step_job(b, s) + (LOOP_JOBS[b] + 2))
                        scores(b, s, u + BANKS)
                        for q in range(G * KB):
                            if unit_of[q * HG + HG - 1] == u:
                                values(b, s, q // KB, q % KB)
                        if u in jobs:
                            jobs[u]()
            pe.wait_ge(acc_free, NCH * G + 1)
            for job in post_jobs(NCH, LAST_POST):
                job()

            def turn_rows(base, r):
                x = base + r
                pe.wait_ge(rows_loaded[r % ROWS_BUFS], base * (16 // ROWS_BUFS) + 16 * (r // ROWS_BUFS + 1))
                pe.wait_ge(turned_taken, x + 1)
                pe.transpose(psum[:, r % 2, 0:P], fr[:, r % ROWS_BUFS, 0:D], ident[:]).then_inc(turned, 1)

            def up(base, r):
                x = base + r
                pe.wait_ge(turned_taken, x + 3)
                pe.wait_ge(staged, x + 1)
                pe.wait_ge(hidden_ready, x + 1)
                for f in range(FC):
                    last = pe.matmul(psum[:, 2 + r % 2, f * P:(f + 1) * P], fw1[:, r % ROWS_BUFS, f * P:(f + 1) * P],
                                     ftt[:, r % 2, :], start=True, stop=True)
                last.then_inc(up_done, 1)

            def down(base, r):
                x = base + r
                pe.wait_ge(gelu_ready, x + 3)
                pe.wait_ge(fo_ready, x + 3)
                for f in range(FC):
                    last = pe.matmul(psum[:, 4 + r % 2, 0:D], fg[:, r % 2, f * P:(f + 1) * P],
                                     fw2[:, r % ROWS_BUFS, f, :], start=(f == 0), stop=(f == FC - 1))
                last.then_inc(down_done, 1)

            turn_rows(0, 0)
            up(0, 0)
            turn_rows(0, 1)
            with pe.Fori(0, NT // ROWS_BUFS) as rnd:
                for r in range(ROWS_BUFS):
                    up(rnd * ROWS_BUFS, r + 1)
                    turn_rows(rnd * ROWS_BUFS, r + 2)
                    down(rnd * ROWS_BUFS, r)


_INS = ['L0_attn_x', 'L0_attn_w_q', 'L0_attn_w_k', 'L0_attn_w_v', 'L0_attn_g_q', 'L0_attn_g_k', 'L0_attn_w_o',
        'L0_attn_b_o', 'L0_attn_gamma', 'L0_attn_beta', 'L0_ffn_switch_w', 'L0_ffn_switch_b', 'L0_ffn_w1',
        'L0_ffn_b1', 'L0_ffn_w2', 'L0_ffn_b2']


def kernel(**inputs):
    import numpy as _np
    import concourse.bacc as _bacc
    from concourse import mybir as _mybir
    from concourse.bass_utils import run_bass_kernel_spmd as _run

    nc = _bacc.Bacc("TRN2", target_bir_lowering=False, num_devices=1)
    arrays, args = {}, []
    for name in _INS:
        a = _np.ascontiguousarray(inputs[name])
        arrays[f"in_{name}_dram"] = a
        args.append(nc.dram_tensor(f"in_{name}_dram", a.shape, _mybir.dt.from_np(a.dtype), kind="ExternalInput").ap())
    shape = arrays["in_L0_attn_x_dram"].shape
    out = nc.dram_tensor("out_0_dram", shape, _mybir.dt.float32, kind="ExternalOutput").ap()
    build(nc, *args, out)
    r = _run(nc, [arrays], core_ids=[0])
    return r.results[0]["out_0_dram"]
```

```python
from contextlib import ExitStack

import concourse.bass as bass
from concourse import mybir

ALU = mybir.AluOpType
ACT = mybir.ActivationFunctionType
AX = mybir.AxisListType
F32 = mybir.dt.float32
F16 = mybir.dt.float16
I32 = mybir.dt.int32

P = 128
CH = 512
TPC = CH // P
HD = 8
HG = 4
QR = P // HG
SHARP = 30.0
THRESHOLD = 0.27
SPLIT = 4096.0
LN_EPS = 1e-5
NORM_EPS2 = 1e-24
RSQRT_SEED = 0x5F3759DF
UNIT = 2
BANKS = 3
RING = 16

J_X1T, J_QK0, J_QK1, J_GDOT, J_V, J_GATE, J_Q, J_K0, J_K1 = range(9)
PROLOGUE_JOBS = 9
J_WO, J_LNT, J_LOGITS, J_RANK = range(4)
POST_JOBS = 4

POST_AT = (5, 15, 17, 38)
PROLOGUE_AT = (49, 56, 58, 60, 62, 82, 83, 85, 87)
ROUTES_AT = 23
GATES_AT = 78
AHEAD = 4
ROWS_BUFS = 8
WORK_BUFS = 4


def unit_plan(tiles):
    plan = [(t, UNIT) for t in range(0, tiles, UNIT)]
    while len(plan) % BANKS:
        at = max(i for i, (_, n) in enumerate(plan) if n == UNIT)
        t = plan[at][0]
        plan[at:at + 1] = [(t, 1), (t + 1, 1)]
    return plan


def build(nc, x, w_q, w_k, w_v, g_q, g_k, w_o, b_o, gamma, beta, switch_w, switch_b, w1, b1, w2, b2, out):
    B, T, D = x.shape
    H = D // HD
    G = H // HG
    E, _, F = w1.shape
    FC = F // P
    N = B * T
    NCH = N // CH
    QC = T // CH
    KB = T // P
    NT = -(-(N // P + E - 1) // ROWS_BUFS) * ROWS_BUFS
    NS = NT + AHEAD
    CAP = N
    MC = CAP // P
    EARLY = QC
    RW = 2 * D + 1
    QS = 2 * HD
    OCT = H * QS // P
    EW = FC * D + FC + D
    SLOTS = E * CAP + NS * P
    TILES = G * KB * HG
    CONSTS = 17
    WEIGHT_LOADS = 10
    PROLOGUE_STEPS = 47
    SPLIT_STEPS = 2
    POST_STEPS = 32
    SCHEDULE_STEPS = 16
    LOOP_STEPS = (POST_STEPS + PROLOGUE_STEPS, POST_STEPS + SCHEDULE_STEPS)
    FULL = 2 * ROWS_BUFS
    assert FULL <= -(-(N - CH - E * (P - 1)) // P)
    NH = 2 * TPC * H
    LOOP_JOBS = (POST_JOBS + PROLOGUE_JOBS, POST_JOBS)
    plan = unit_plan(TILES)
    U = len(plan)
    GROUP_END = [sum(t0 < (g + 1) * KB * HG for t0, _ in plan) for g in range(G)]
    unit_of = {t: u for u, (t0, n) in enumerate(plan) for t in range(t0, t0 + n)}

    x_tok = x.rearrange("b t d -> (b t) d")
    out_tok = out.rearrange("b t d -> (b t) d")

    with ExitStack() as ctx:
        def sb(name, shape, dt=F32):
            return ctx.enter_context(nc.sbuf_tensor(name, shape, dt))

        def sem(name):
            return ctx.enter_context(nc.semaphore(name))

        q_dram = nc.dram_tensor("q_split", (NCH * H * QS, CH), F16, kind="Internal").ap()
        gate_dram = nc.dram_tensor("q_gates", (NCH * H, CH), F32, kind="Internal").ap()
        rows_dram = nc.dram_tensor("token_rows", (N, RW), F32, kind="Internal").ap()
        slot_dram = nc.dram_tensor("slot_token", (SLOTS, 1), I32, kind="Internal").ap()

        psum = ctx.enter_context(nc.psum_tensor("psum", [P, 8, CH], F32))
        acc = psum[:, 6, :]
        misc = psum[:, 7, :]
        misc16 = misc.bitcast(F16)

        ident = sb("ident", [P, P])
        ident16 = sb("ident16", [P, P], F16)
        upper = sb("upper", [P, P])
        ones = sb("ones", [P, P])
        iota_e = sb("iota_e", [P, E])
        iota_m = sb("iota_m", [P, MC])
        iota_t = sb("iota_t", [P, NS])
        iota_p = sb("iota_p", [P, 1])
        warm = sb("warm", [P, 1])
        no_token = sb("no_token", [P, NS], I32)
        tok_step = sb("tok_step", [P, TPC], I32)
        tok_i = sb("tok_i", [P, NCH * TPC], I32)
        gam = sb("gam", [P, 1])
        bet = sb("bet", [P, 1])
        bet_rep = sb("bet_rep", [P, P])
        wqk = sb("wqk", [P, 2, D])
        wqk_g = sb("wqk_g", [P, 2, D])
        wv = sb("wv", [P, D])
        wo = sb("wo", [P, D])
        own_rows = sb("own_rows", [P, G])
        ident_sums = sb("ident_sums", [P, HG, G])
        g_heads = sb("g_heads", [P, 2, HD])
        bo = sb("bo", [P, D])
        sw = sb("sw", [P, E])
        swb = sb("swb", [P, E])
        qk_beta = sb("qk_beta", [P, 2, D])
        w_gate = sb("w_gate", [P, 2 * H])
        gate_beta = sb("gate_beta", [P, 2 * H])

        xres = sb("xres", [P, (NCH + 1) * TPC * D])
        kw = sb("kw", [P, NCH * G * CH], F16)
        vw = sb("vw", [P, NCH * TPC * D])

        st = sb("st", [P, QC * TPC, 6])
        mv = sb("mv", [P, QC * TPC, 2])
        var4 = sb("var4", [P, QC * TPC])
        var_eps = sb("var_eps", [P, QC * TPC])
        rs4 = sb("rs4", [P, QC * TPC])
        rs_again = sb("rs_again", [P, QC * TPC])
        nt_a = sb("nt_a", [P, QC * 2 * TPC * H])
        nt_b = sb("nt_b", [P, QC * 2 * TPC * H])
        x1 = sb("x1", [P, TPC, D])
        x1t = sb("x1t", [P, CH])
        qk = sb("qk", [P, 2, TPC, D])
        qkn = sb("qkn", [P, 2, TPC, D])
        ss = sb("ss", [P, QC * 2 * TPC * H])
        inv = sb("inv", [P, QC * 2 * TPC * H])
        gsum = sb("gsum", [P, QC * 2 * TPC * H])
        gdot = sb("gdot", [P, QC * TPC, 2 * H])
        gates = sb("gates", [P, 2, TPC, H])
        qs = sb("qs", [P, TPC * H, 2, HD], F16)
        ks = sb("ks", [P, TPC * H, 4, HD], F16)
        qt = sb("qt", [P, OCT, CH], F16)
        gate_t = sb("gate_t", [H, CH])

        qm = sb("qm", [P, H, CH], F16)
        gt = sb("gt", [P, CH])
        ring = sb("ring", [P, RING, CH])
        ft = sb("ft", [P, CH])

        rows = sb("rows", [P, TPC, RW])
        tt = sb("tt", [P, CH])
        lg = sb("lg", [P, TPC, E])
        lmax = sb("lmax", [P, TPC])
        sp_ = sb("sig_pos", [P, TPC, E])
        sn_ = sb("sig_neg", [P, TPC, E])
        ex = sb("ex", [P, TPC, E])
        emax = sb("emax", [P, TPC])
        esum = sb("esum", [P, TPC])
        cand = sb("cand", [P, TPC, E])
        route = sb("route", [P, TPC])
        onehot = sb("onehot", [P, TPC, E])
        rank = sb("rank", [P, 2, TPC, E])
        run = sb("run", [P, E])
        live = sb("live", [P, 1])
        slot_f = sb("slot_f", [P, TPC])
        slot_i = sb("slot_i", [P, TPC], I32)

        grid = sb("grid", [P, E, MC])
        tiles_e = sb("tiles_e", [P, E])
        full_run = sb("full_run", [P, E])
        done_e = sb("done_e", [P, E])
        picked = sb("picked", [P, NS, E])
        done_s = sb("done_s", [P, NS])
        cum_e = sb("cum_e", [P, E])
        part_e = [sb(f"part_e{i}", [P, E]) for i in range(2)]
        started = sb("started", [P, NS, E])
        began = sb("began", [P, NS, E])
        tile_e = sb("tile_e", [P, NS])
        tile_s = sb("tile_s", [P, NS])
        first_slot = sb("first_slot", [P, NS], I32)
        eid = sb("eid", [P, NS], I32)
        ids = [sb(f"ids{r}", [P, 1], I32) for r in range(ROWS_BUFS)]

        ring_flat = ring[:].rearrange("p r n -> p (r n)")
        taken = [0]

        def after_ring(*shape):
            size = 1
            for n in shape:
                size *= n
            at = taken[0]
            taken[0] += size
            assert taken[0] <= RING * CH
            names = "abc"[:len(shape)]
            pattern = f"p ({' '.join(names)}) -> p {' '.join(names)}"
            return ring_flat[:, at:at + size].rearrange(pattern, **dict(zip(names, shape)))

        x1_early = ring_flat[:, 0:QC * CH].rearrange("p (t d) -> p t d", d=D)
        x1t_early = ring_flat[:, QC * CH:2 * QC * CH].rearrange("p (c n) -> p c n", c=QC)
        qk_early = ring_flat[:, 2 * QC * CH:4 * QC * CH]
        squares_early = kw[:, EARLY * G * CH:].bitcast(F32)

        fr = qm[:].rearrange("p h n -> p (h n)").bitcast(F32)[:, 0:ROWS_BUFS * RW].rearrange("p (r w) -> p r w", w=RW)
        fw1 = after_ring(WORK_BUFS, F)
        stage = after_ring(WORK_BUFS, EW)
        fw2 = stage[:, :, 0:FC * D].rearrange("p r (c d) -> p r c d", c=FC)
        fb1 = stage[:, :, FC * D:FC * D + FC]
        fb2 = stage[:, :, FC * D + FC:EW]
        w1_all = kw[:, 0:NCH // B * G * CH].bitcast(F32)
        assert NCH // B * G * CH // 2 >= E * F
        experts = sb("experts", [P, E * EW])
        fo = sb("fo", [P, WORK_BUFS, D])
        ftt = after_ring(2, P)
        fh = after_ring(2, FC * P)
        fg = after_ring(2, FC * P)

        loaded_x = [sem(f"loaded_x{c}") for c in range(T // CH)]
        loaded_late = sem("loaded_late")
        loaded_w = sem("loaded_w")
        const_made = sem("const_made")
        tok_copied = sem("tok_copied")
        loaded_wo = sem("loaded_wo")
        no_token_made = sem("no_token_made")
        pool_turns = sem("pool_turns")
        rows_free = sem("rows_free")
        slots_cleared = sem("slots_cleared")
        weights_made = sem("weights_made")
        gate_weights_made = sem("gate_weights_made")
        misc_full = sem("misc_full")
        misc_free = sem("misc_free")
        vec = sem("vector_step")
        x1_ready = sem("x1_ready")
        proj_full = sem("projections_full")
        proj_free = sem("projections_free")
        value_full = sem("values_full")
        value_free = sem("values_free")
        turn_full = sem("turns_full")
        turn_free = sem("turns_free")
        norm_ready = sem("norm_ready")
        squares_ready = sem("squares_ready")
        gsum_ready = sem("gsum_ready")
        gsig_ready = sem("gsig_ready")
        gates_ready = sem("gates_ready")
        qs_ready = sem("qs_ready")
        ks_ready = sem("ks_ready")
        q_stored = sem("q_stored")
        gate_stored = sem("gate_stored")
        q_loaded = [sem(f"q_loaded{g}") for g in range(G)]
        gt_loaded = sem("gt_loaded")
        qm_cleared = sem("qm_cleared")
        scores_ready = sem("scores_ready")
        sig_done = sem("sig_done")
        pv_done = sem("pv_done")
        acc_free = sem("acc_free")
        ft_ready = sem("ft_ready")
        t_ready = sem("t_ready")
        d_ready = sem("d_ready")
        esig_ready = sem("esig_ready")
        onehot_ready = sem("onehot_ready")
        row_ready = sem("row_ready")
        rows_stored = sem("rows_stored")
        slots_stored = sem("slots_stored")
        sched_ready = sem("sched_ready")
        ids_loaded = [sem(f"ids_loaded{r}") for r in range(ROWS_BUFS)]
        rows_loaded = [sem(f"rows_loaded{r}") for r in range(ROWS_BUFS)]
        experts_loaded = sem("experts_loaded")
        act_turns = sem("act_turns")
        staged = sem("staged")
        ids_cleared = sem("ids_cleared")
        sp_turns = sem("sp_turns")
        turned = sem("rows_turned")
        turned_taken = sem("turned_rows_taken")
        up_done = sem("up_done")
        hidden_ready = sem("hidden_ready")
        gelu_ready = sem("gelu_ready")
        down_done = sem("down_done")
        fo_ready = sem("fo_ready")
        out_stored = [sem(f"out_stored{r}") for r in range(ROWS_BUFS)]


        def step_job(b, s):
            done = b * QC * LOOP_JOBS[0]
            return (s - b * QC) * LOOP_JOBS[b] + done

        LAST_POST = QC * (LOOP_JOBS[0] + LOOP_JOBS[1])

        T_Q, T_K0, T_K1, T_GATE = range(4)
        TURNS = 4
        TURN_BANK = (4, 0, 1, 5)

        def turns_before(c, j):
            return c * TURNS + (EARLY + j)

        block = ctx.enter_context(nc.Block())

        @block.sync
        def _(sp):
            for c in range(NCH):
                src = x_tok[c * CH:(c + 1) * CH, :].rearrange("(t p) d -> p t d", p=P)
                dst = xres[:, (c + 1) * CH:(c + 2) * CH].rearrange("p (t d) -> p t d", t=TPC)
                sp.dma_start(dst, src).then_inc(loaded_x[c] if c < EARLY else loaded_late, 16)

            def store_gates(c, evacuated, at):
                sp.wait_ge(evacuated, at)
                sp.dma_start(gate_dram[bass.ds(c * H, H), :], gate_t[:]).then_inc(gate_stored, 16)

            def store_queries(c, evacuated, at):
                sp.wait_ge(evacuated, at)
                sp.dma_start(q_dram[bass.ds(c * (H * QS), H * QS), :].rearrange("(o p) n -> p o n", p=P),
                             qt[:]).then_inc(q_stored, 16)

            def load_q(s, g):
                for j in range(HG):
                    for half in range(2):
                        r0 = QR * j + QS * half
                        sp.dma_start(qm[r0:r0 + QS, g * HG + j, :],
                                     q_dram[bass.ds(s * (H * QS) + (g * HG + j) * QS, QS), :]).then_inc(q_loaded[g], 16)

            def head_rows(g, j):
                return slice(QR * j + HD * g, QR * j + HD * (g + 1))

            def load_gates(s):
                for g in range(G):
                    for j in range(HG):
                        sp.dma_start(gt[head_rows(g, j), :],
                                     gate_dram[bass.ds(s * H + (g * HG + j), 1), :].to_broadcast([HD, CH])
                                     ).then_inc(gt_loaded, 16)

            for g in range(G):
                for j in range(HG):
                    h = g * HG + j
                    sp.dma_start(wo[head_rows(g, j), :], w_o[h * HD:(h + 1) * HD, :]).then_inc(loaded_wo, 16)

            for c in range(max(EARLY, G)):
                if c < EARLY:
                    store_queries(c, turn_free, turns_before(c, T_Q) + 1)
                    store_gates(c, turn_free, turns_before(c, T_GATE) + 1)
                if c == 0:
                    sp.wait_ge(q_stored, 32)
                    sp.wait_ge(qm_cleared, 1)
                if c < G:
                    load_q(0, c)
            sp.wait_ge(gate_stored, 16 * (EARLY + 1))
            load_gates(0)

            by_expert = experts[:].rearrange("p (e n) -> p e n", e=E)
            for e in range(E):
                sp.dma_start(by_expert[:, e, 0:FC * D].rearrange("p (c d) -> p c d", c=FC),
                             w2[e].rearrange("(c p) d -> p c d", p=P)).then_inc(experts_loaded, 16)
                for c in range(FC):
                    sp.dma_start(by_expert[:, e, FC * D + c:FC * D + c + 1],
                                 b1[e, c * P:(c + 1) * P].rearrange("(p a) -> p a", a=1)).then_inc(experts_loaded, 16)
                sp.dma_start(by_expert[:, e, FC * D + FC:EW],
                             b2[e:e + 1, :].to_broadcast([P, D])).then_inc(experts_loaded, 16)

            def load_step(s, g):
                sp.wait_ge(scores_ready, s * U + (GROUP_END[g] - U))
                load_q(s, g)
                if g == G - 1:
                    sp.wait_ge(ft_ready, s + 1)
                    load_gates(s)

            with sp.Fori(1, QC + 1) as s:
                sp.wait_ge(q_stored, s * 16 + 32)
                sp.wait_ge(gate_stored, s * 16 + 32)
                for g in range(G - 1):
                    load_step(s, g)
                job = step_job(0, s - 1) + POST_JOBS
                store_gates(s + (QC - 1), misc_free, job + (J_GATE + 3))
                store_queries(s + (QC - 1), misc_free, job + (J_Q + 3))
                load_step(s, G - 1)
            for e in range(E):
                sp.dma_start(w1_all[:, e * F:(e + 1) * F], w1[e]).then_inc(experts_loaded, 16)
            with sp.Fori(QC + 1, NCH) as s:
                sp.wait_ge(q_stored, s * 16 + 32)
                sp.wait_ge(gate_stored, s * 16 + 32)
                for g in range(G):
                    load_step(s, g)
            sp.wait_ge(scores_ready, (NCH - 1) * U + GROUP_END[0])
            load_q(NCH - 1, 0)

            def wait(sem_, value):
                sp.wait_ge(sem_, value)
                sp.sem_inc(sp_turns, 1)

            def fetch(base, r):
                x = base + r
                wait(out_stored[r], base * (16 // ROWS_BUFS) + 16)
                slot = sp.value_load(first_slot[0:1, bass.ds(x, 1)], min_val=0, max_val=SLOTS - P)
                sp.dma_start(ids[r][:], slot_dram[bass.ds(slot, P), :]).then_inc(ids_loaded[r], 16)

            sp.wait_ge(acc_free, (NCH - 1) * G + 3)
            sp.wait_ge(rows_free, NCH + 1)
            with sp.Fori(0, FULL // ROWS_BUFS) as rnd:
                for r in range(ROWS_BUFS):
                    fetch(rnd * ROWS_BUFS, r)
            sp.wait_ge(rows_free, NCH + 2)
            sp.wait_ge(sched_ready, 1)
            with sp.Fori(FULL // ROWS_BUFS, NT // ROWS_BUFS) as rnd:
                for r in range(ROWS_BUFS):
                    fetch(rnd * ROWS_BUFS, r)
            for r in range(AHEAD):
                fetch(NT, r)

        @block.gpsimd
        def _(pool):
            made = [0]

            def make(ins):
                made[0] += 1
                ins.then_inc(const_made, 1)

            make(pool.memset(ident[:], 0.0))
            make(pool.memset(ident16[:], 0.0))
            make(pool.memset(upper[:], 0.0))
            pool.wait_ge(const_made, made[0])
            for m in (ident, ident16):
                make(pool.affine_select(out=m[:], in_=m[:], compare_op=ALU.not_equal, fill=1.0, base=0,
                                        pattern=[[-1, P]], channel_multiplier=1))
            make(pool.affine_select(out=upper[:], in_=upper[:], compare_op=ALU.is_ge, fill=1.0, base=0,
                                    pattern=[[-1, P]], channel_multiplier=1))
            make(pool.memset(ones[:], 1.0))
            make(pool.iota(iota_e[:], pattern=[[1, E]], base=0, channel_multiplier=0,
                           allow_small_or_imprecise_dtypes=True))
            make(pool.iota(iota_m[:], pattern=[[P, MC]], base=0, channel_multiplier=0,
                           allow_small_or_imprecise_dtypes=True))
            make(pool.iota(iota_t[:], pattern=[[1, NS]], base=0, channel_multiplier=0,
                           allow_small_or_imprecise_dtypes=True))
            make(pool.iota(iota_p[:], pattern=[[0, 1]], base=0, channel_multiplier=1,
                           allow_small_or_imprecise_dtypes=True))
            make(pool.iota(tok_i[:], pattern=[[P, NCH * TPC]], base=0, channel_multiplier=1))
            make(pool.memset(xres[:, 0:CH], 0.0))
            make(pool.memset(ft[:], 0.0))
            make(pool.memset(run[:], 0.0))
            make(pool.memset(live[:], 0.0))
            make(pool.memset(rows[:], 0.0))
            assert made[0] == CONSTS
            pool.memset(qm[:], 0.0).then_inc(qm_cleared, 1)
            pool.memset(no_token[:], N).then_inc(no_token_made, 1)
            pool.wait_ge(no_token_made, 1)
            for i in range(0, SLOTS // P, NS):
                n = min(NS, SLOTS // P - i)
                pool.dma_start(slot_dram[i * P:(i + n) * P, :].rearrange("(p n) c -> p (n c)", p=P),
                               no_token[:, 0:n]).then_inc(slots_cleared, 16)
            pool.wait_ge(slots_cleared, 16 * len(range(0, SLOTS // P, NS)))

            def wait(sem_, value):
                pool.wait_ge(sem_, value)
                pool.sem_inc(pool_turns, 1)

            def scatter(r):
                pool.indirect_dma_start(out_tok[:, :], bass.IndirectOffsetOnAxis(ap=ids[r][:], axis=0),
                                        fo[:, r % WORK_BUFS, :], None,
                                        bounds_check=N - 1, oob_is_err=False).then_inc(out_stored[r], 16)

            for r in range(ROWS_BUFS):
                pool.memset(ids[r][:], N).then_inc(ids_cleared, 1)
            pool.memset(fo[:], 0.0).then_inc(ids_cleared, 1)
            pool.wait_ge(ids_cleared, ROWS_BUFS + 1)
            for r in range(ROWS_BUFS):
                scatter(r)

            def store_rows(c):
                wait(row_ready, c + 2)
                pool.tensor_copy(tok_step[:], tok_i[:, bass.ds(c * TPC, TPC)]).then_inc(tok_copied, 1)
                wait(tok_copied, c + 1)
                pool.dma_start(rows_dram[bass.ds(c * CH, CH), :].rearrange("(t p) w -> p t w", p=P),
                               rows[:]).then_inc(rows_stored, 16)
                for t in range(TPC):
                    pool.indirect_dma_start(slot_dram[:, :], bass.IndirectOffsetOnAxis(ap=slot_i[:, t:t + 1], axis=0),
                                            tok_step[:, t:t + 1], None).then_inc(slots_stored, 16)

            def finish_rows(c):
                wait(rows_stored, c * 16 + 16)
                wait(slots_stored, c * (16 * TPC) + 16 * TPC)
                pool.sem_inc(rows_free, 1)

            with pool.Fori(0, NCH - 1) as c:
                store_rows(c)
                finish_rows(c)
            def gather(base, r, tokens=N):
                wait(ids_loaded[r % ROWS_BUFS], base * (16 // ROWS_BUFS) + 16 * (r // ROWS_BUFS + 1))
                pool.indirect_dma_start(fr[:, r % ROWS_BUFS, :], None, rows_dram[0:tokens, :],
                                        bass.IndirectOffsetOnAxis(ap=ids[r % ROWS_BUFS][:], axis=0),
                                        bounds_check=tokens - 1, oob_is_err=False
                                        ).then_inc(rows_loaded[r % ROWS_BUFS], 16)

            assert FULL >= ROWS_BUFS
            pool.wait_ge(acc_free, NCH * G + 1)
            for r in range(AHEAD):
                gather(0, r, N - CH)
            for x in range(FULL):
                gather(0, x + AHEAD, N - CH if x + AHEAD < FULL else N)
                wait(fo_ready, x + 1 + WORK_BUFS)
                scatter(x % ROWS_BUFS)
                if x == 3:
                    store_rows(NCH - 1)
                if x == 6:
                    finish_rows(NCH - 1)
            with pool.Fori(FULL // ROWS_BUFS, NT // ROWS_BUFS) as rnd:
                for r in range(ROWS_BUFS):
                    gather(rnd * ROWS_BUFS, r + AHEAD)
                    wait(fo_ready, rnd * ROWS_BUFS + (r + 1 + WORK_BUFS))
                    scatter(r)
            for r in range(ROWS_BUFS):
                wait(out_stored[r], 16 * (NT + ROWS_BUFS) // ROWS_BUFS)

        @block.scalar
        def _(act):
            act.dma_start(gam[:], gamma.rearrange("(p a) -> p a", a=1)).then_inc(loaded_w, 16)
            act.dma_start(bet[:], beta.rearrange("(p a) -> p a", a=1)).then_inc(loaded_w, 16)
            act.dma_start(wqk[:, 0, :], w_q).then_inc(loaded_w, 16)
            act.dma_start(wqk[:, 1, :], w_k).then_inc(loaded_w, 16)
            act.dma_start(wv[:], w_v).then_inc(loaded_w, 16)
            for a, g_vec in enumerate((g_q, g_k)):
                act.dma_start(g_heads[:, a, :], g_vec.rearrange("(a d) -> a d", a=1).to_broadcast([P, HD])
                              ).then_inc(loaded_w, 16)
            act.dma_start(bo[:], b_o.rearrange("(a d) -> a d", a=1).to_broadcast([P, D])).then_inc(loaded_w, 16)
            act.dma_start(sw[:], switch_w).then_inc(loaded_w, 16)
            act.dma_start(swb[:], switch_b.rearrange("(a d) -> a d", a=1).to_broadcast([P, E])).then_inc(loaded_w, 16)
            act.wait_ge(const_made, CONSTS)
            act.activation(warm[:], iota_p[:], ACT.Sigmoid)
            for c in range(EARLY):
                act.wait_ge(turn_full, c + 1)
                act.activation(x1t_early[:, c, :], psum[:, c % 2, :], ACT.Copy).then_inc(turn_free, 1)
            with act.Fori(0, EARLY) as c:
                act.wait_ge(proj_free, c * 3 + 6)
                act.activation(squares_early[:, bass.ds(c * 2 * CH, 2 * CH)], qk_early[:, bass.ds(c * 2 * CH, 2 * CH)],
                               ACT.Square).then_inc(squares_ready, 1)
            with act.Fori(0, EARLY) as c:
                act.wait_ge(gsum_ready, c + 1)
                chunk_gates = gsum[:, bass.ds(c * NH, NH)]
                act.activation(chunk_gates, chunk_gates, ACT.Sigmoid, scale=1.0 / SPLIT).then_inc(gsig_ready, 1)
                act.wait_ge(q_stored, c * 16 + 16)
                kc = kw[:, bass.ds(c * (G * CH), G * CH)].rearrange("p (g n) -> p g n", g=G)
                act.wait_ge(turn_full, turns_before(c, T_Q) + 1)
                act.activation(qt[:].rearrange("p o n -> p (o n)"), psum[:, TURN_BANK[T_Q], :].bitcast(F16),
                               ACT.Copy).then_inc(turn_free, 1)
                for half, j in enumerate((T_K0, T_K1)):
                    act.wait_ge(turn_full, turns_before(c, j) + 1)
                    act.activation(kc[:, :, 2 * P * half:2 * P * (half + 1)].rearrange("p g (t n) -> p t g n", t=2),
                                   psum[:, TURN_BANK[j], :].bitcast(F16).rearrange("p (t g n) -> p t g n", t=2, g=G),
                                   ACT.Copy).then_inc(turn_free, 1)
                act.wait_ge(turn_full, turns_before(c, T_GATE) + 1)
                act.wait_ge(gate_stored, c * 16 + 16)
                act.activation(gate_t[:], psum[0:H, TURN_BANK[T_GATE], :], ACT.Copy).then_inc(turn_free, 1)

            def units(s, lo, hi):
                for u in range(lo, hi):
                    t0, n = plan[u]
                    act.wait_ge(scores_ready, s * U + (u + 1))
                    kb_last = (t0 + n - 1 - RING) // HG
                    act.wait_ge(pv_done, s * (G * KB) + (kb_last + 1 + G * KB))
                    r0, b0 = t0 % RING, u % BANKS * UNIT
                    act.activation(ring[:, r0:r0 + n, :], psum[:, b0:b0 + n, :], ACT.Sigmoid,
                               scale=SHARP / SPLIT ** 2, bias=-SHARP * THRESHOLD).then_inc(sig_done, 1)

            for b in range(B):
                with act.Fori(b * QC, (b + 1) * QC) as s:
                    units(s, 0, ROUTES_AT)
                    act.wait_ge(d_ready, s + 1)
                    act.activation(sp_[:], lg[:], ACT.Sigmoid)
                    act.activation(sn_[:], lg[:], ACT.Sigmoid, scale=-1.0).then_inc(esig_ready, 1)
                    units(s, ROUTES_AT, GATES_AT)
                    if b + 1 < B:
                        act.wait_ge(gsum_ready, s + (EARLY + 1))
                        act.activation(gsum[:, 0:NH], gsum[:, 0:NH], ACT.Sigmoid, scale=1.0 / SPLIT).then_inc(gsig_ready, 1)
                    units(s, GATES_AT, U)
            def stage_weights(x, r):
                act.wait_ge(fo_ready, x + 1)
                act.sem_inc(act_turns, 1)
                e = act.value_load(eid[0:1, bass.ds(x, 1)], min_val=0, max_val=E - 1)
                act.activation(fw1[:, r, :], w1_all[:, bass.ds(e * F, F)], ACT.Copy)
                act.activation(stage[:, r, :], experts[:, bass.ds(e * EW, EW)], ACT.Copy).then_inc(staged, 1)

            act.wait_ge(experts_loaded, 16 * E * (FC + 3))
            act.wait_ge(acc_free, NCH * G + 1)
            for r in range(2):
                stage_weights(r, r)
            act.wait_ge(d_ready, NCH + 1)
            act.activation(sp_[:], lg[:], ACT.Sigmoid)
            act.activation(sn_[:], lg[:], ACT.Sigmoid, scale=-1.0).then_inc(esig_ready, 1)
            act.activation(warm[:], iota_p[:], ACT.Gelu_apprx_tanh)

            def gelu_tile(x, r):
                act.wait_ge(hidden_ready, x + 3)
                act.wait_ge(down_done, x + 1)
                act.activation(fg[:, r % 2, :], fh[:, r % 2, :], ACT.Gelu_apprx_tanh).then_inc(gelu_ready, 1)
                stage_weights(x + 2, (r + 2) % WORK_BUFS)

            for x in range(ROWS_BUFS):
                gelu_tile(x, x)
            act.wait_ge(sched_ready, 1)
            with act.Fori(ROWS_BUFS // WORK_BUFS, NT // WORK_BUFS) as rnd:
                for r in range(WORK_BUFS):
                    gelu_tile(rnd * WORK_BUFS + r, r)

        @block.vector
        def _(dve):
            steps = [0]

            def link(ins, base=0):
                steps[0] += 1
                ins.then_inc(vec, 1)
                dve.wait_ge(vec, base + steps[0])

            def rsqrt(y, a, t, u, base):
                link(dve.tensor_scalar(t.bitcast(I32), a.bitcast(I32), 1, None, ALU.logical_shift_right), base)
                link(dve.tensor_scalar(y.bitcast(I32), t.bitcast(I32), -1.0, float(RSQRT_SEED), ALU.mult, ALU.add), base)
                for _ in range(3):
                    link(dve.scalar_tensor_tensor(t, y, -0.5, y, ALU.mult, ALU.mult), base)
                    link(dve.tensor_tensor(u, t, a, ALU.mult), base)
                    link(dve.scalar_tensor_tensor(y, u, 1.5, y, ALU.add, ALU.mult), base)

            def statistics(src, n, base, loaded=None):
                for t in range(n):
                    if loaded and t % TPC == 0:
                        dve.wait_ge(loaded[t // TPC], 16)
                    last = dve.bn_stats(st[:, t, :], src[:, t, :])
                link(last, base)
                m_e, m_o, v_e, v_o = st[:, 0:n, 1], st[:, 0:n, 4], st[:, 0:n, 2], st[:, 0:n, 5]
                mean, diff, var = mv[:, 0:n, 0], mv[:, 0:n, 1], var4[:, 0:n]
                dve.tensor_tensor(mean, m_e, m_o, ALU.add)
                dve.tensor_tensor(diff, m_e, m_o, ALU.subtract)
                link(dve.tensor_tensor(var, v_e, v_o, ALU.add), base)
                dve.tensor_scalar(mean, mean, 0.5, None, ALU.mult)
                link(dve.scalar_tensor_tensor(diff, diff, 0.25, diff, ALU.mult, ALU.mult), base)
                link(dve.scalar_tensor_tensor(var, var, 1.0 / D, diff, ALU.mult, ALU.add), base)
                link(dve.tensor_scalar(var_eps[:, 0:n], var, LN_EPS, None, ALU.add), base)
                rsqrt(rs4[:, 0:n], var_eps[:, 0:n], nt_a[:, 0:n], nt_b[:, 0:n], base)

            def normalise(dst, src, lo, hi):
                for t in range(lo, hi):
                    last = dve.tensor_scalar(dst[:, t, :], src[:, t, :], mv[:, t, 0:1], rs4[:, t:t + 1],
                                             ALU.subtract, ALU.mult)
                return last

            def layernorm(dst, src, base):
                statistics(src, TPC, base)
                return normalise(dst, src, 0, TPC)

            def factor_again(n, base):
                var = var4[:, 0:n]
                link(dve.tensor_tensor(var, var, rs4[:, 0:n], ALU.mult), base)
                link(dve.tensor_tensor(var, var, rs4[:, 0:n], ALU.mult), base)
                link(dve.tensor_scalar(var, var, LN_EPS, None, ALU.add), base)
                rsqrt(rs_again[:, 0:n], var, nt_a[:, 0:n], nt_b[:, 0:n], base)

            dve.sem_inc(misc_free, 1)
            dve.sem_inc(acc_free, 1)
            dve.sem_inc(pv_done, G * KB)
            dve.sem_inc(q_stored, 16)
            dve.sem_inc(gate_stored, 16)
            dve.sem_inc(rows_free, 2)
            dve.sem_inc(fo_ready, WORK_BUFS)
            dve.sem_inc(proj_free, 3)
            dve.sem_inc(value_free, 1)
            for s_ in (turned_taken, up_done, hidden_ready, gelu_ready, down_done):
                dve.sem_inc(s_, 2)
            dve.sem_inc(ft_ready, 1)
            qk_flat = qk[:].rearrange("p a t d -> p (a t d)")
            qkn_h = qkn[:].rearrange("p a t (h d) -> p (a t h) d", d=HD)

            def take_qk(dst, half, bank, factor):
                for t in range(2):
                    tile = 2 * half + t
                    last = dve.scalar_tensor_tensor(dst.rearrange("p (a t d) -> p a t d", a=2, t=TPC)[:, :, tile, :],
                                                    bank[:, t * 2 * D:(t + 1) * 2 * D].rearrange("p (a d) -> p a d", a=2),
                                                    factor[:, tile:tile + 1], qk_beta[:], ALU.mult, ALU.add)
                return last

            def take_gdot(dst, bank, factor):
                return dve.tensor_tensor(dst, bank[:, 0:NH].rearrange("p (t n) -> p t n", t=TPC),
                                         factor[:, 0:TPC].unsqueeze(2).to_broadcast([P, TPC, 2 * H]), ALU.mult)

            def square_sums(dst, src, base):
                src_h = src.rearrange("p (n d) -> p n d", d=HD)
                link(dve.tensor_tensor(qkn_h, src_h, src_h, ALU.mult), base)
                link(dve.tensor_reduce(dst, qkn_h, AX.X, ALU.add), base)

            def inverse_norms(n, base):
                link(dve.tensor_scalar(ss[:, 0:n], ss[:, 0:n], NORM_EPS2, 1.0 / SPLIT ** 2, ALU.max, ALU.mult), base)
                rsqrt(inv[:, 0:n], ss[:, 0:n], nt_a[:, 0:n], nt_b[:, 0:n], base)

            def gate_arguments(chunks, base):
                tiles = gdot[:, 0:chunks * TPC, :]
                link(dve.tensor_tensor(tiles, tiles, gate_beta[:].unsqueeze(1).to_broadcast([P, chunks * TPC, 2 * H]),
                                       ALU.add), base)
                for c in range(chunks):
                    view = lambda ap: ap[:, c * NH:(c + 1) * NH].rearrange("p (a t h) -> p t a h", a=2, t=TPC)
                    dve.tensor_tensor(view(gsum),
                                      gdot[:, c * TPC:(c + 1) * TPC, :].rearrange("p t (a h) -> p t a h", a=2),
                                      view(inv), ALU.mult).then_inc(gsum_ready, 1)

            def scale_heads(c, src, factor):
                dve.tensor_tensor(qkn_h, src.rearrange("p (n d) -> p n d", d=HD),
                                  factor.unsqueeze(2).to_broadcast([P, NH, HD]), ALU.mult).then_inc(norm_ready, 1)
                dve.wait_ge(norm_ready, c + 1)

            q3 = qkn[:, 0].rearrange("p t (h d) -> p (t h) d", d=HD)
            k3 = qkn[:, 1].rearrange("p t (h d) -> p (t h) d", d=HD)

            def leading_parts(base):
                dve.tensor_copy(qs[:, :, 0, :], q3)
                for i in (0, 1):
                    last = dve.tensor_copy(ks[:, :, i, :], k3)
                link(last, base)

            def trailing_parts(base):
                dve.tensor_tensor(qs[:, :, 1, :], q3, qs[:, :, 0, :], ALU.subtract).then_inc(qs_ready, 1)
                link(dve.tensor_tensor(ks[:, :, 2, :], k3, ks[:, :, 0, :], ALU.subtract), base)
                dve.tensor_copy(ks[:, :, 3, :], ks[:, :, 2, :]).then_inc(ks_ready, 1)

            def gate_values(c, bank, sigmoids):
                dve.wait_ge(gsig_ready, c + 1)
                dve.tensor_scalar(gates[:].rearrange("p a t h -> p (a t h)"), sigmoids, 0.75, 0.25,
                                  ALU.mult, ALU.add).then_inc(gates_ready, 1)
                dve.wait_ge(gates_ready, c + 1)

                def take():
                    for t in range(TPC):
                        last = dve.tensor_tensor(
                            vw[:, bass.ds(c * CH + t * D, D)].rearrange("p (j g d) -> p j g d", j=HG, g=G),
                            bank[:, t * D:(t + 1) * D].rearrange("p (g j d) -> p j g d", g=G, j=HG),
                            gates[:, 1, t, :].rearrange("p (g j) -> p j g", g=G).unsqueeze(3)
                            .to_broadcast([P, HG, G, HD]), ALU.mult)
                    return last

                return take

            x_early = xres[:, CH:(EARLY + 1) * CH].rearrange("p (t d) -> p t d", d=D)
            statistics(x_early, EARLY * TPC, 0, loaded_x)
            for c in range(EARLY):
                normalise(x1_early, x_early, c * TPC, (c + 1) * TPC).then_inc(x1_ready, 1)
            dve.wait_ge(loaded_w, 16 * WEIGHT_LOADS)
            dve.wait_ge(const_made, CONSTS)
            dve.tensor_scalar(bet_rep[:], ones[:], bet[:], None, ALU.mult)
            dve.tensor_scalar(wqk_g[:].rearrange("p a d -> p (a d)"), wqk[:].rearrange("p a d -> p (a d)"), gam[:],
                              None, ALU.mult).then_inc(weights_made, 1)

            def fold_gate(dst, src):
                for a in range(2):
                    last = dve.tensor_tensor(qkn[:, a, 0, :].rearrange("p (h d) -> p h d", d=HD),
                                             src[:, a, :].rearrange("p (h d) -> p h d", d=HD),
                                             g_heads[:, a, :].unsqueeze(1).to_broadcast([P, H, HD]), ALU.mult)
                link(last)
                link(dve.tensor_reduce(dst[:].rearrange("p (a h) -> p a h", a=2),
                                       qkn[:, :, 0, :].rearrange("p a (h d) -> p a h d", d=HD), AX.X, ALU.add))

            dve.wait_ge(weights_made, 1)
            fold_gate(w_gate, wqk_g)
            dve.sem_inc(gate_weights_made, 1)
            link(dve.tensor_reduce(ident_sums[:], ident[:].rearrange("p (j g d) -> p j g d", j=HG, g=G), AX.X, ALU.add))
            link(dve.tensor_reduce(own_rows[:], ident_sums[:].rearrange("p j g -> p g j"), AX.X, ALU.add))
            factor_again(EARLY * TPC, 0)
            dve.wait_ge(misc_full, 1)
            dve.tensor_copy(qk_beta[:].rearrange("p a d -> p (a d)"), misc[:, 0:2 * D]).then_inc(misc_free, 1)
            dve.wait_ge(misc_free, 2)
            fold_gate(gate_beta, qk_beta)
            dve.wait_ge(loaded_late, 16 * (NCH - EARLY))
            base0 = 0

            def project_early(c):
                chunk, factor = qk_early[:, c * 2 * CH:(c + 1) * 2 * CH], rs_again[:, c * TPC:(c + 1) * TPC]
                for half in range(2):
                    dve.wait_ge(proj_full, c * 3 + (half + 1))
                    take_qk(chunk, half, psum[:, 2 + half, :], factor).then_inc(proj_free, 1)
                dve.wait_ge(proj_full, c * 3 + 3)
                take_gdot(gdot[:, c * TPC:(c + 1) * TPC, :], acc, factor).then_inc(proj_free, 1)

            def sum_squares_early(c):
                dve.wait_ge(squares_ready, c + 1)
                link(dve.tensor_reduce(ss[:, c * NH:(c + 1) * NH],
                                       squares_early[:, c * 2 * CH:(c + 1) * 2 * CH].rearrange("p (n d) -> p n d", d=HD),
                                       AX.X, ALU.add))

            def split_early(c, base):
                scale_heads(c, qk_early[:, bass.ds(c * 2 * CH, 2 * CH)], inv[:, bass.ds(c * NH, NH)])
                dve.wait_ge(turn_full, turns_before(c, T_Q) - (TURNS - 1 - T_K1))
                leading_parts(base)
                trailing_parts(base)
                take = gate_values(c, misc, gsum[:, bass.ds(c * NH, NH)])
                dve.wait_ge(value_full, c + 1)
                take().then_inc(value_free, 1)

            for c in range(EARLY):
                project_early(c)
                if c > 0:
                    sum_squares_early(c - 1)
            sum_squares_early(EARLY - 1)
            dve.wait_ge(proj_free, 3 * EARLY + 3)
            inverse_norms(EARLY * NH, base0)
            gate_arguments(EARLY, base0)
            n0 = steps[0]
            with dve.Fori(0, EARLY) as c:
                split_early(c, c * SPLIT_STEPS + base0)
            assert steps[0] - n0 == SPLIT_STEPS, steps[0] - n0
            base0 += (EARLY - 1) * SPLIT_STEPS

            def prologue_parts(c, base, first_job):
                return (lambda: front(c, base, first_job)), (lambda: back(c, base, first_job))

            def front(c, base, first_job):
                job = lambda j: first_job + (j + 2)
                xc = xres[:, bass.ds(c * CH + CH, CH)].rearrange("p (t d) -> p t d", t=TPC)
                layernorm(x1, xc, base).then_inc(x1_ready, 1)
                factor_again(TPC, base)
                dve.wait_ge(misc_full, job(J_X1T))
                dve.tensor_copy(x1t[:], misc).then_inc(misc_free, 1)
                for half, j in ((0, J_QK0), (1, J_QK1)):
                    dve.wait_ge(misc_full, job(j))
                    take_qk(qk_flat, half, misc, rs_again).then_inc(misc_free, 1)
                dve.wait_ge(misc_full, job(J_GDOT))
                take_gdot(gdot[:, 0:TPC, :], misc, rs_again).then_inc(misc_free, 1)

            def back(c, base, first_job):
                job = lambda j: first_job + (j + 2)
                dve.wait_ge(misc_free, job(J_GDOT) + 1)
                square_sums(ss[:, 0:NH], qk_flat, base)
                inverse_norms(NH, base)
                gate_arguments(1, base)
                scale_heads(c, qk_flat, inv[:, 0:NH])
                leading_parts(base)
                trailing_parts(base)
                take = gate_values(c, misc, gsum[:, 0:NH])
                dve.wait_ge(misc_full, job(J_V))
                take().then_inc(misc_free, 1)
                dve.wait_ge(misc_full, job(J_GATE))
                dve.wait_ge(gate_stored, c * 16 + 16)
                dve.tensor_copy(gate_t[:], misc[0:H, :]).then_inc(misc_free, 1)
                dve.wait_ge(misc_full, job(J_Q))
                dve.wait_ge(q_stored, c * 16 + 16)
                dve.tensor_copy(qt[:].rearrange("p o n -> p (o n)"), misc16).then_inc(misc_free, 1)
                kc = kw[:, bass.ds(c * (G * CH), G * CH)].rearrange("p (g n) -> p g n", g=G)
                for half, j in ((0, J_K0), (1, J_K1)):
                    dve.wait_ge(misc_full, job(j))
                    dve.tensor_copy(kc[:, :, 2 * P * half:2 * P * (half + 1)].rearrange("p g (t n) -> p t g n", t=2),
                                    misc16.rearrange("p (t g n) -> p t g n", t=2, g=G)).then_inc(misc_free, 1)

            def take_group(s, g):
                dve.wait_ge(pv_done, s * (G * KB) + (G * KB + KB * (g + 1)))
                if g == 0:
                    dve.tensor_scalar(ft[:], acc, own_rows[:, 0:1], None, ALU.mult).then_inc(acc_free, 1)
                else:
                    dve.scalar_tensor_tensor(ft[:], acc, own_rows[:, g:g + 1], ft[:], ALU.mult,
                                             ALU.add).then_inc(acc_free, 1)
                dve.wait_ge(acc_free, s * G + (g + 2))
                if g == G - 1:
                    dve.wait_ge(gt_loaded, s * (16 * H) + 16 * H)
                    dve.tensor_tensor(ft[:], ft[:], gt[:], ALU.mult).then_inc(ft_ready, 1)

            def post_parts(s, base, first_job):
                job = lambda j: first_job + (j + 2)
                x2 = rows[:, :, D:2 * D]
                tn = rows[:, :, 0:D]
                xc = xres[:, bass.ds(s * CH, CH)].rearrange("p (t d) -> p t d", t=TPC)

                def residual():
                    dve.wait_ge(rows_free, s + 1)
                    link(dve.tensor_tensor(x2, xc, bo[:].unsqueeze(1).to_broadcast([P, TPC, D]), ALU.add), base)
                    dve.wait_ge(misc_full, job(J_WO))
                    dve.tensor_tensor(x2, x2, misc.rearrange("p (t d) -> p t d", t=TPC), ALU.add).then_inc(misc_free, 1)
                    dve.wait_ge(misc_free, job(J_WO) + 1)
                    layernorm(tn, x2, base).then_inc(t_ready, 1)

                def logits():
                    dve.wait_ge(misc_full, job(J_LNT))
                    dve.tensor_copy(tt[:], misc).then_inc(misc_free, 1)
                    dve.wait_ge(misc_full, job(J_LOGITS))
                    dve.tensor_tensor(lg[:], misc[:, 0:TPC * E].rearrange("p (t e) -> p t e", e=E),
                                      swb[:].unsqueeze(1).to_broadcast([P, TPC, E]), ALU.add).then_inc(misc_free, 1)
                    dve.wait_ge(misc_free, job(J_LOGITS) + 1)
                    link(dve.tensor_reduce(lmax[:], lg[:], AX.X, ALU.max), base)
                    dve.tensor_tensor(lg[:], lg[:], lmax[:].unsqueeze(2).to_broadcast([P, TPC, E]),
                                      ALU.subtract).then_inc(d_ready, 1)

                def routes():
                    dve.wait_ge(esig_ready, s + 1)
                    link(dve.reciprocal(sn_[:], sn_[:]), base)
                    link(dve.tensor_tensor(ex[:], sp_[:], sn_[:], ALU.mult), base)
                    dve.tensor_reduce(esum[:], ex[:], AX.X, ALU.add)
                    link(dve.tensor_reduce(emax[:], ex[:], AX.X, ALU.max), base)
                    dve.tensor_tensor(cand[:], ex[:], emax[:].unsqueeze(2).to_broadcast([P, TPC, E]), ALU.is_ge)
                    link(dve.reciprocal(esum[:], esum[:]), base)
                    dve.tensor_tensor(rows[:, :, 2 * D:RW], emax[:].unsqueeze(2), esum[:].unsqueeze(2), ALU.mult)
                    link(dve.scalar_tensor_tensor(cand[:], cand[:], -float(E),
                                                  iota_e[:].unsqueeze(1).to_broadcast([P, TPC, E]),
                                                  ALU.mult, ALU.add), base)
                    link(dve.tensor_reduce(route[:], cand[:], AX.X, ALU.min), base)
                    link(dve.tensor_scalar(route[:], route[:], float(E), None, ALU.add), base)
                    dve.tensor_tensor(onehot[:], iota_e[:].unsqueeze(1).to_broadcast([P, TPC, E]),
                                      route[:].unsqueeze(2).to_broadcast([P, TPC, E]),
                                      ALU.is_equal).then_inc(onehot_ready, 1)
                    dve.wait_ge(onehot_ready, s + 1)

                def ranks():
                    dve.wait_ge(misc_full, job(J_RANK))
                    dve.tensor_copy(rank[:].rearrange("p a t e -> p (a t e)"),
                                    misc[:, 0:2 * TPC * E]).then_inc(misc_free, 1)
                    dve.wait_ge(misc_free, job(J_RANK) + 1)
                    for t in range(TPC):
                        dve.tensor_tensor(rank[:, 0, t, :], rank[:, 0, t, :], run[:], ALU.add)
                        link(dve.tensor_tensor(run[:], run[:], rank[:, 1, t, :], ALU.add), base)
                    link(dve.tensor_tensor(rank[:, 0], rank[:, 0], onehot[:], ALU.mult), base)
                    link(dve.tensor_reduce(slot_f[:], rank[:, 0], AX.X, ALU.add), base)
                    dve.tensor_scalar(run[:], run[:], live[:], None, ALU.mult)
                    link(dve.scalar_tensor_tensor(slot_f[:], route[:], float(CAP), slot_f[:], ALU.mult, ALU.add), base)
                    dve.memset(live[:], 1.0)
                    dve.tensor_copy(slot_i[:], slot_f[:]).then_inc(row_ready, 1)
                    dve.wait_ge(row_ready, s + 1)

                return residual, logits, routes, ranks

            b3 = lambda ap, shape, at: ap.unsqueeze(at).to_broadcast(shape)

            def schedule(counts, lo, hi, base):
                n = hi - lo
                tile_i, tile_x, start = iota_t[:, 0:n], tile_e[:, 0:n], tile_s[:, 0:n]
                link(dve.tensor_tensor(grid[:], b3(counts, [P, E, MC], 2), b3(iota_m[:], [P, E, MC], 1), ALU.is_gt), base)
                link(dve.tensor_reduce(tiles_e[:], grid[:], AX.X, ALU.add), base)
                if lo:
                    link(dve.tensor_tensor(tiles_e[:], tiles_e[:], done_e[:], ALU.subtract), base)
                shifts = [1 << i for i in range((E - 1).bit_length())]
                bufs = [tiles_e] + [part_e[i % 2] for i in range(len(shifts) - 1)] + [cum_e]
                for shift, src, dst in zip(shifts, bufs, bufs[1:]):
                    dve.tensor_copy(dst[:, 0:shift], src[:, 0:shift])
                    link(dve.tensor_tensor(dst[:, shift:E], src[:, shift:E], src[:, 0:E - shift], ALU.add), base)
                link(dve.tensor_tensor(started[:, 0:n, :], b3(cum_e[:], [P, n, E], 1), b3(tile_i, [P, n, E], 2),
                                       ALU.is_le), base)
                dve.tensor_reduce(tile_x, started[:, 0:n, :], AX.X, ALU.add)
                link(dve.tensor_tensor(began[:, 0:n, :], started[:, 0:n, :], b3(tiles_e[:], [P, n, E], 1),
                                       ALU.mult), base)
                link(dve.tensor_reduce(start, began[:, 0:n, :], AX.X, ALU.add), base)
                link(dve.tensor_tensor(start, tile_i, start, ALU.subtract), base)
                if lo:
                    link(dve.tensor_tensor(picked[:, 0:n, :], b3(iota_e[:], [P, n, E], 1), b3(tile_x, [P, n, E], 2),
                                           ALU.is_equal), base)
                    link(dve.tensor_tensor(picked[:, 0:n, :], picked[:, 0:n, :], b3(done_e[:], [P, n, E], 1),
                                           ALU.mult), base)
                    link(dve.tensor_reduce(done_s[:, 0:n], picked[:, 0:n, :], AX.X, ALU.add), base)
                    link(dve.tensor_tensor(start, start, done_s[:, 0:n], ALU.add), base)
                link(dve.tensor_scalar(start, start, float(P), None, ALU.mult), base)
                link(dve.scalar_tensor_tensor(start, tile_x, float(CAP), start, ALU.mult, ALU.add), base)
                dve.tensor_copy(first_slot[:, lo:hi], start)
                link(dve.tensor_scalar(eid[:, lo:hi], tile_x, float(E - 1), None, ALU.min), base)

            def schedule_full(base):
                n0 = steps[0]
                link(dve.tensor_scalar(full_run[:], run[:], 1.0 - P, None, ALU.add), base)
                schedule(full_run[:], 0, FULL, base)
                link(dve.tensor_tensor(done_e[:], cum_e[:], tiles_e[:], ALU.subtract), base)
                link(dve.tensor_scalar(done_e[:], done_e[:], -1.0, float(FULL), ALU.mult, ALU.add), base)
                link(dve.scalar_tensor_tensor(done_e[:], done_e[:], 0.0, tiles_e[:], ALU.max, ALU.min), base)
                assert steps[0] - n0 == SCHEDULE_STEPS, steps[0] - n0

            for b in range(B):
                with dve.Fori(b * QC, (b + 1) * QC) as s:
                    n0 = steps[0]
                    base = (s - b * QC) * LOOP_STEPS[b] + base0
                    residual, logits, routes, ranks = post_parts(s, base, step_job(b, s))
                    residual()
                    logits()
                    routes()
                    take_group(s, 0)
                    ranks()
                    if b + 1 < B:
                        make, finish = prologue_parts(s + EARLY, base, step_job(b, s) + POST_JOBS)
                        make()
                        take_group(s, 1)
                        finish()
                    else:
                        schedule_full(base)
                        take_group(s, 1)
                    take_group(s, 2)
                    take_group(s, 3)
                    assert steps[0] - n0 == LOOP_STEPS[b], steps[0] - n0
                base0 += (QC - 1) * LOOP_STEPS[b]
            def add_b1(base, r):
                x = base + r
                r4 = r % WORK_BUFS
                dve.wait_ge(up_done, x + 3)
                dve.wait_ge(staged, x + 1)
                dve.wait_ge(gelu_ready, x + 1)
                dve.tensor_tensor(fh[:, r % 2, :].rearrange("p (c n) -> p c n", c=FC),
                                  psum[:, 2 + r % 2, :].rearrange("p (c n) -> p c n", c=FC),
                                  fb1[:, r4, :].unsqueeze(2).to_broadcast([P, FC, P]), ALU.add).then_inc(hidden_ready, 1)

            def take_turned(base, r):
                x = base + r
                dve.wait_ge(turned, x + 1)
                dve.wait_ge(up_done, x + 1)
                dve.tensor_copy(ftt[:, r % 2, :], psum[:, r % 2, 0:P]).then_inc(turned_taken, 1)

            def finish_tile(base, r, stored, link_base):
                x, r4 = base + r, r % WORK_BUFS
                add_b1(base, r + 1)
                take_turned(base, r + 2)
                dve.wait_ge(down_done, x + 3)
                dve.wait_ge(rows_loaded[r], base * (16 // ROWS_BUFS) + 16)
                dve.wait_ge(out_stored[(r + WORK_BUFS) % ROWS_BUFS], stored)
                link(dve.tensor_tensor(fo[:, r4, :], psum[:, 4 + r % 2, 0:D], fb2[:, r4, :], ALU.add), link_base)
                dve.scalar_tensor_tensor(fo[:, r4, :], fo[:, r4, :], fr[:, r, 2 * D:RW], fr[:, r, D:2 * D],
                                         ALU.mult, ALU.add).then_inc(fo_ready, 1)

            residual, logits, routes, ranks = post_parts(NCH, base0, LAST_POST)
            residual()
            logits()
            take_turned(0, 0)
            take_turned(0, 1)
            add_b1(0, 0)
            between = {0: routes, 1: ranks}
            for r in range(ROWS_BUFS):
                finish_tile(0, r, 16 if r < WORK_BUFS else 32, base0)
                if r in between:
                    between[r]()
                if r == 5:
                    schedule(run[:], FULL, NS, base0)
                    dve.sem_inc(sched_ready, 1)
            n0 = steps[0]
            with dve.Fori(1, NT // ROWS_BUFS) as rnd:
                for r in range(ROWS_BUFS):
                    finish_tile(rnd * ROWS_BUFS, r, rnd * 16 + (16 if r < WORK_BUFS else 32),
                                (rnd - 1) * ROWS_BUFS + base0)
            assert steps[0] - n0 == ROWS_BUFS, steps[0] - n0

        @block.tensor
        def _(pe):
            pe.wait_ge(const_made, CONSTS)
            def turn_tokens(bank, src):
                for t in range(TPC):
                    last = pe.transpose(bank[:, t * P:(t + 1) * P], src[:, t, :], ident[:])
                return last

            def make_qk(bank, turned_x, half):
                for t in range(2):
                    tile = 2 * half + t
                    last = pe.matmul(bank[:, t * 2 * D:(t + 1) * 2 * D], turned_x[:, tile * P:(tile + 1) * P],
                                     wqk_g[:].rearrange("p a d -> p (a d)"), start=True, stop=True)
                return last

            def make_gdot(bank, turned_x):
                for t in range(TPC):
                    last = pe.matmul(bank[:, t * 2 * H:(t + 1) * 2 * H], turned_x[:, t * P:(t + 1) * P], w_gate[:],
                                     start=True, stop=True)
                return last

            def make_v(bank, turned_x):
                for t in range(TPC):
                    last = pe.matmul(bank[:, t * D:(t + 1) * D], turned_x[:, t * P:(t + 1) * P], wv[:],
                                     start=True, stop=True)
                return last

            def turn_gates(bank, c):
                pe.wait_ge(gates_ready, c + 1)
                for t in range(TPC):
                    last = pe.transpose(bank[0:H, t * P:(t + 1) * P], gates[:, 0, t, :], ident[:])
                return last

            def turn_queries(bank):
                bank16, heads = bank.bitcast(F16), P // QS
                for o in range(OCT):
                    for t in range(TPC):
                        r0 = t * H + o * heads
                        last = pe.transpose(bank16[:, o * CH + t * P:o * CH + (t + 1) * P],
                                            qs[:, r0:r0 + heads, :, :].rearrange("p h c d -> p (h c d)"), ident16[:])
                return last

            def turn_keys(bank, half):
                bank16 = bank.bitcast(F16)
                for t in range(2):
                    for g in range(G):
                        r0 = (2 * half + t) * H + g * HG
                        at = (t * G + g) * P
                        last = pe.transpose(bank16[:, at:at + P],
                                            ks[:, r0:r0 + HG, :, :].rearrange("p h c d -> p (h c d)"), ident16[:])
                return last

            for c in range(EARLY):
                pe.wait_ge(x1_ready, c + 1)
                if c >= 2:
                    pe.wait_ge(turn_free, c - 1)
                turn_tokens(psum[:, c % 2, :], x1_early[:, c * TPC:(c + 1) * TPC, :]).then_inc(turn_full, 1)

            pe.wait_ge(weights_made, 1)
            pe.wait_ge(misc_free, 1)
            pe.matmul(misc[:, 0:2 * D], bet_rep[:], wqk[:].rearrange("p a d -> p (a d)"),
                      start=True, stop=True).then_inc(misc_full, 1)

            def x1t_of(c):
                return ring_flat[:, QC * CH + c * CH:QC * CH + (c + 1) * CH]

            def project_early(c):
                pe.wait_ge(turn_free, c + 1)
                for j in range(3):
                    pe.wait_ge(proj_free, c * 3 + (j + 1))
                    if j < 2:
                        last = make_qk(psum[:, 2 + j, :], x1t_of(c), j)
                    else:
                        pe.wait_ge(gate_weights_made, 1)
                        last = make_gdot(acc, x1t_of(c))
                    last.then_inc(proj_full, 1)

            def turn_early(c):
                pe.wait_ge(value_free, c + 1)
                make_v(misc, x1t_of(c)).then_inc(value_full, 1)
                pe.wait_ge(turn_free, turns_before(c, T_Q))
                pe.wait_ge(qs_ready, c + 1)
                turn_queries(psum[:, TURN_BANK[T_Q], :]).then_inc(turn_full, 1)
                pe.wait_ge(ks_ready, c + 1)
                turn_keys(psum[:, TURN_BANK[T_K0], :], 0).then_inc(turn_full, 1)
                turn_keys(psum[:, TURN_BANK[T_K1], :], 1).then_inc(turn_full, 1)
                turn_gates(psum[:, TURN_BANK[T_GATE], :], c).then_inc(turn_full, 1)

            for c in range(EARLY):
                project_early(c)
            for c in range(EARLY):
                turn_early(c)

            pe.wait_ge(turn_free, turns_before(EARLY, 0))
            pe.wait_ge(proj_free, 3 * EARLY + 3)
            pe.wait_ge(value_free, EARLY + 1)
            pe.wait_ge(loaded_wo, 16 * H)

            def prologue_jobs(c, first_job):
                def free(j):
                    pe.wait_ge(misc_free, first_job + (j + 2))

                def turn_x1():
                    pe.wait_ge(x1_ready, c + 1)
                    free(J_X1T)
                    turn_tokens(misc, x1).then_inc(misc_full, 1)

                def project(half):
                    free((J_QK0, J_QK1)[half])
                    make_qk(misc, x1t, half).then_inc(misc_full, 1)

                def gdot_job():
                    free(J_GDOT)
                    make_gdot(misc, x1t).then_inc(misc_full, 1)

                def v_job():
                    free(J_V)
                    make_v(misc, x1t).then_inc(misc_full, 1)

                def gates_job():
                    free(J_GATE)
                    turn_gates(misc, c).then_inc(misc_full, 1)

                def queries_job():
                    pe.wait_ge(qs_ready, c + 1)
                    free(J_Q)
                    turn_queries(misc).then_inc(misc_full, 1)

                def keys_job(half):
                    pe.wait_ge(ks_ready, c + 1)
                    free((J_K0, J_K1)[half])
                    turn_keys(misc, half).then_inc(misc_full, 1)

                return (turn_x1, lambda: project(0), lambda: project(1), gdot_job, v_job, gates_job,
                        queries_job, lambda: keys_job(0), lambda: keys_job(1))

            def scores(b, s, u):
                over, v = divmod(u, U)
                t0, n = plan[v]
                if s is not None:
                    pe.wait_ge(sig_done, s * U + (u - BANKS + 1))
                for i in range(n):
                    g, kb, j = (t0 + i) // (KB * HG), (t0 + i) // HG % KB, (t0 + i) % HG
                    if (t0 + i) % (KB * HG) == 0:
                        loads = 16 * 2 * HG
                        first = loads * (1 + over)
                        pe.wait_ge(q_loaded[g], first if s is None else s * loads + first)
                    at = ((b * QC + kb // TPC) * G + g) * CH + kb % TPC * P
                    keys = kw[:, at:at + P]
                    if over and b + 1 < B:
                        keys = kw[:, bass.ds((s + 1) // QC * (QC * G * CH) + at, P)]
                    last = pe.matmul(psum[:, u % BANKS * UNIT + i, :], keys, qm[:, g * HG + j, :],
                                     start=True, stop=True)
                last.then_inc(scores_ready, 1)

            def values(b, s, g, kb):
                pe.wait_ge(sig_done, s * U + (unit_of[(g * KB + kb) * HG + HG - 1] + 1))
                if kb == 0:
                    pe.wait_ge(acc_free, s * G + (g + 1))
                for j in range(HG):
                    tile = (g * KB + kb) * HG + j
                    at = (b * KB + kb) * D + j * QR
                    last = pe.matmul(acc[QR * j:QR * (j + 1), :], vw[:, at:at + QR],
                                     ring[:, tile % RING, :],
                                     start=(kb == 0), stop=(kb == KB - 1), tile_position=(0, QR * j))
                last.then_inc(pv_done, 1)

            def post_jobs(s, first_job):
                def free(j):
                    pe.wait_ge(misc_free, first_job + (j + 2))

                def project():
                    free(J_WO)
                    pe.wait_ge(ft_ready, s + 1)
                    for t in range(TPC):
                        last = pe.matmul(misc[:, t * D:(t + 1) * D], ft[:, t * P:(t + 1) * P], wo[:],
                                         start=True, stop=True)
                    last.then_inc(misc_full, 1)

                def turn():
                    pe.wait_ge(t_ready, s + 1)
                    free(J_LNT)
                    for t in range(TPC):
                        last = pe.transpose(misc[:, t * P:(t + 1) * P], rows[:, t, 0:D], ident[:])
                    last.then_inc(misc_full, 1)

                def route():
                    free(J_LOGITS)
                    for t in range(TPC):
                        last = pe.matmul(misc[:, t * E:(t + 1) * E], tt[:, t * P:(t + 1) * P], sw[:],
                                         start=True, stop=True)
                    last.then_inc(misc_full, 1)

                def count():
                    pe.wait_ge(onehot_ready, s + 1)
                    free(J_RANK)
                    oh = onehot[:].rearrange("p t e -> p (t e)")
                    pe.matmul(misc[:, 0:TPC * E], upper[:], oh, start=True, stop=True)
                    pe.matmul(misc[:, TPC * E:2 * TPC * E], ones[:], oh, start=True, stop=True).then_inc(misc_full, 1)

                return project, turn, route, count

            for u in range(BANKS):
                scores(0, None, u)
            for b in range(B):
                with pe.Fori(b * QC, (b + 1) * QC) as s:
                    jobs = dict(zip(POST_AT, post_jobs(s, step_job(b, s))))
                    if b + 1 < B:
                        jobs.update(zip(PROLOGUE_AT, prologue_jobs(s + EARLY, step_job(b, s) + POST_JOBS)))
                    for u in range(U):
                        if u == U - BANKS:
                            pe.wait_ge(misc_free, step_job(b, s) + (LOOP_JOBS[b] + 2))
                        scores(b, s, u + BANKS)
                        for q in range(G * KB):
                            if unit_of[q * HG + HG - 1] == u:
                                values(b, s, q // KB, q % KB)
                        if u in jobs:
                            jobs[u]()
            pe.wait_ge(acc_free, NCH * G + 1)
            def turn_rows(base, r):
                x = base + r
                pe.wait_ge(rows_loaded[r % ROWS_BUFS], base * (16 // ROWS_BUFS) + 16 * (r // ROWS_BUFS + 1))
                pe.wait_ge(turned_taken, x + 1)
                pe.transpose(psum[:, r % 2, 0:P], fr[:, r % ROWS_BUFS, 0:D], ident[:]).then_inc(turned, 1)

            def up(base, r):
                x = base + r
                pe.wait_ge(turned_taken, x + 3)
                pe.wait_ge(staged, x + 1)
                pe.wait_ge(hidden_ready, x + 1)
                for f in range(FC):
                    last = pe.matmul(psum[:, 2 + r % 2, f * P:(f + 1) * P], fw1[:, r % WORK_BUFS, f * P:(f + 1) * P],
                                     ftt[:, r % 2, :], start=True, stop=True)
                last.then_inc(up_done, 1)

            def down(base, r):
                x = base + r
                pe.wait_ge(gelu_ready, x + 3)
                pe.wait_ge(fo_ready, x + 3)
                for f in range(FC):
                    last = pe.matmul(psum[:, 4 + r % 2, 0:D], fg[:, r % 2, f * P:(f + 1) * P],
                                     fw2[:, r % WORK_BUFS, f, :], start=(f == 0), stop=(f == FC - 1))
                last.then_inc(down_done, 1)

            def expert_tile(base, r):
                up(base, r + 1)
                turn_rows(base, r + 2)
                down(base, r)

            project, turn, route, count = post_jobs(NCH, LAST_POST)
            project()
            turn()
            route()
            turn_rows(0, 0)
            up(0, 0)
            turn_rows(0, 1)
            for r in range(ROWS_BUFS):
                expert_tile(0, r)
                if r == 1:
                    count()
            with pe.Fori(1, NT // ROWS_BUFS) as rnd:
                for r in range(ROWS_BUFS):
                    expert_tile(rnd * ROWS_BUFS, r)


_INS = ['L0_attn_x', 'L0_attn_w_q', 'L0_attn_w_k', 'L0_attn_w_v', 'L0_attn_g_q', 'L0_attn_g_k', 'L0_attn_w_o',
        'L0_attn_b_o', 'L0_attn_gamma', 'L0_attn_beta', 'L0_ffn_switch_w', 'L0_ffn_switch_b', 'L0_ffn_w1',
        'L0_ffn_b1', 'L0_ffn_w2', 'L0_ffn_b2']


def kernel(**inputs):
    import numpy as _np
    import concourse.bacc as _bacc
    from concourse import mybir as _mybir
    from concourse.bass_utils import run_bass_kernel_spmd as _run

    nc = _bacc.Bacc("TRN2", target_bir_lowering=False, num_devices=1)
    arrays, args = {}, []
    for name in _INS:
        a = _np.ascontiguousarray(inputs[name])
        arrays[f"in_{name}_dram"] = a
        args.append(nc.dram_tensor(f"in_{name}_dram", a.shape, _mybir.dt.from_np(a.dtype), kind="ExternalInput").ap())
    shape = arrays["in_L0_attn_x_dram"].shape
    out = nc.dram_tensor("out_0_dram", shape, _mybir.dt.float32, kind="ExternalOutput").ap()
    build(nc, *args, out)
    r = _run(nc, [arrays], core_ids=[0])
    return r.results[0]["out_0_dram"]
```
